# Optimizing a Trainium2 kernel written in Bass

```python
import numpy as np
import jax
import jax.numpy as jnp

def _softmax(x, axis=-1):
    return jax.nn.softmax(x, axis=axis)

def _gelu(x):
    return jax.nn.gelu(x, approximate=True)

def _silu(x):
    return jax.nn.silu(x)

def _sigmoid(x):
    return jax.nn.sigmoid(x)

def _layernorm(x, axis=-1, eps=1e-05):
    m = jnp.mean(x, axis=axis, keepdims=True)
    v = jnp.var(x, axis=axis, keepdims=True)
    return (x - m) / jnp.sqrt(v + eps)

def _scatter_add(tgt, idx, src, axis=0):
    return tgt.at[idx].add(src)

def _segment_sum(src, seg, n):
    return jax.ops.segment_sum(src, seg, n)
kernel_name = 'mk_dlrm_tower_d1_rec_r8_1f33e9'

def setup_inputs(seed: int=0):
    np.random.seed(seed)
    _w = jnp.asarray

    def _rec_inputs():
        import jax
        import jax.numpy as jnp
        _tk = jax.random.key(seed)
        dense_ctx = jax.random.normal(jax.random.fold_in(_tk, 190), (512, 16), jnp.float32)
        ids = jnp.stack([jax.random.randint(jax.random.fold_in(_tk, 200 + f), (512,), 0, v, jnp.int32) for f, v in enumerate([1250, 1250, 1250, 125000, 1000, 125000, 1000, 1000, 1250, 1000, 1000, 125000, 12500, 125000, 1000, 1000, 12500, 1250, 1250, 1250, 1000, 12500, 12500, 1250, 125000, 12500, 125000, 1250, 1250, 12500, 1250, 1250])], axis=1)
        tbl_0 = 0.05 * jax.random.normal(jax.random.fold_in(_tk, 500 + 0), (1250, 16), jnp.float32)
        tbl_1 = 0.05 * jax.random.normal(jax.random.fold_in(_tk, 500 + 1), (1250, 16), jnp.float32)
        tbl_2 = 0.05 * jax.random.normal(jax.random.fold_in(_tk, 500 + 2), (1250, 16), jnp.float32)
        tbl_3 = 0.05 * jax.random.normal(jax.random.fold_in(_tk, 500 + 3), (125000, 16), jnp.float32)
        tbl_4 = 0.05 * jax.random.normal(jax.random.fold_in(_tk, 500 + 4), (1000, 16), jnp.float32)
        tbl_5 = 0.05 * jax.random.normal(jax.random.fold_in(_tk, 500 + 5), (125000, 16), jnp.float32)
        tbl_6 = 0.05 * jax.random.normal(jax.random.fold_in(_tk, 500 + 6), (1000, 16), jnp.float32)
        tbl_7 = 0.05 * jax.random.normal(jax.random.fold_in(_tk, 500 + 7), (1000, 16), jnp.float32)
        tbl_8 = 0.05 * jax.random.normal(jax.random.fold_in(_tk, 500 + 8), (1250, 16), jnp.float32)
        tbl_9 = 0.05 * jax.random.normal(jax.random.fold_in(_tk, 500 + 9), (1000, 16), jnp.float32)
        tbl_10 = 0.05 * jax.random.normal(jax.random.fold_in(_tk, 500 + 10), (1000, 16), jnp.float32)
        tbl_11 = 0.05 * jax.random.normal(jax.random.fold_in(_tk, 500 + 11), (125000, 16), jnp.float32)
        tbl_12 = 0.05 * jax.random.normal(jax.random.fold_in(_tk, 500 + 12), (12500, 16), jnp.float32)
        tbl_13 = 0.05 * jax.random.normal(jax.random.fold_in(_tk, 500 + 13), (125000, 16), jnp.float32)
        tbl_14 = 0.05 * jax.random.normal(jax.random.fold_in(_tk, 500 + 14), (1000, 16), jnp.float32)
        tbl_15 = 0.05 * jax.random.normal(jax.random.fold_in(_tk, 500 + 15), (1000, 16), jnp.float32)
        tbl_16 = 0.05 * jax.random.normal(jax.random.fold_in(_tk, 500 + 16), (12500, 16), jnp.float32)
        tbl_17 = 0.05 * jax.random.normal(jax.random.fold_in(_tk, 500 + 17), (1250, 16), jnp.float32)
        tbl_18 = 0.05 * jax.random.normal(jax.random.fold_in(_tk, 500 + 18), (1250, 16), jnp.float32)
        tbl_19 = 0.05 * jax.random.normal(jax.random.fold_in(_tk, 500 + 19), (1250, 16), jnp.float32)
        tbl_20 = 0.05 * jax.random.normal(jax.random.fold_in(_tk, 500 + 20), (1000, 16), jnp.float32)
        tbl_21 = 0.05 * jax.random.normal(jax.random.fold_in(_tk, 500 + 21), (12500, 16), jnp.float32)
        tbl_22 = 0.05 * jax.random.normal(jax.random.fold_in(_tk, 500 + 22), (12500, 16), jnp.float32)
        tbl_23 = 0.05 * jax.random.normal(jax.random.fold_in(_tk, 500 + 23), (1250, 16), jnp.float32)
        tbl_24 = 0.05 * jax.random.normal(jax.random.fold_in(_tk, 500 + 24), (125000, 16), jnp.float32)
        tbl_25 = 0.05 * jax.random.normal(jax.random.fold_in(_tk, 500 + 25), (12500, 16), jnp.float32)
        tbl_26 = 0.05 * jax.random.normal(jax.random.fold_in(_tk, 500 + 26), (125000, 16), jnp.float32)
        tbl_27 = 0.05 * jax.random.normal(jax.random.fold_in(_tk, 500 + 27), (1250, 16), jnp.float32)
        tbl_28 = 0.05 * jax.random.normal(jax.random.fold_in(_tk, 500 + 28), (1250, 16), jnp.float32)
        tbl_29 = 0.05 * jax.random.normal(jax.random.fold_in(_tk, 500 + 29), (12500, 16), jnp.float32)
        tbl_30 = 0.05 * jax.random.normal(jax.random.fold_in(_tk, 500 + 30), (1250, 16), jnp.float32)
        tbl_31 = 0.05 * jax.random.normal(jax.random.fold_in(_tk, 500 + 31), (1250, 16), jnp.float32)
        _rk = jax.random.fold_in(_tk, 7)
        W_top1 = 0.0693375 * jax.random.normal(jax.random.fold_in(_tk, 801), (208, 512), jnp.float32)
        W_top2 = 0.0441942 * jax.random.normal(jax.random.fold_in(_tk, 802), (512, 256), jnp.float32)
        W_top3 = 0.0625 * jax.random.normal(jax.random.fold_in(_tk, 803), (256, 1), jnp.float32)
        b_top1 = jnp.zeros((512,), jnp.float32)
        b_top2 = jnp.zeros((256,), jnp.float32)
        return (dense_ctx, ids, tbl_0, tbl_1, tbl_2, tbl_3, tbl_4, tbl_5, tbl_6, tbl_7, tbl_8, tbl_9, tbl_10, tbl_11, tbl_12, tbl_13, tbl_14, tbl_15, tbl_16, tbl_17, tbl_18, tbl_19, tbl_20, tbl_21, tbl_22, tbl_23, tbl_24, tbl_25, tbl_26, tbl_27, tbl_28, tbl_29, tbl_30, tbl_31, W_top1, b_top1, W_top2, b_top2, W_top3)
    dense_ctx, ids, tbl_0, tbl_1, tbl_2, tbl_3, tbl_4, tbl_5, tbl_6, tbl_7, tbl_8, tbl_9, tbl_10, tbl_11, tbl_12, tbl_13, tbl_14, tbl_15, tbl_16, tbl_17, tbl_18, tbl_19, tbl_20, tbl_21, tbl_22, tbl_23, tbl_24, tbl_25, tbl_26, tbl_27, tbl_28, tbl_29, tbl_30, tbl_31, W_top1, b_top1, W_top2, b_top2, W_top3 = _rec_inputs()

    def _L0_rec_setup():
        import jax, jax.numpy as jnp
        import numpy as np
        B, M, D = (2048, 32, 16)
        LAYERS = [64, 64, 64]
        key = jax.random.key(seed)
        ks = jax.random.split(key, 4)
        inp = {'embeddings': jax.random.normal(ks[0], (B, M, D), dtype=jnp.float32)}
        hk_1 = M
        for i, hk in enumerate(LAYERS):
            scale = (2.0 / (M * hk_1 + hk)) ** 0.5
            inp[f'W{i}'] = jax.random.normal(ks[i + 1], (M, hk_1, hk), dtype=jnp.float32) * scale
            hk_1 = hk
        return inp
    _L0_rec_all = _L0_rec_setup()
    _L0_rec_in = {k: v for k, v in _L0_rec_all.items() if k in ('W0', 'W1', 'W2')}
    del _L0_rec_all
    return {'dense_ctx': dense_ctx, 'ids': ids, 'tbl_0': tbl_0, 'tbl_1': tbl_1, 'tbl_2': tbl_2, 'tbl_3': tbl_3, 'tbl_4': tbl_4, 'tbl_5': tbl_5, 'tbl_6': tbl_6, 'tbl_7': tbl_7, 'tbl_8': tbl_8, 'tbl_9': tbl_9, 'tbl_10': tbl_10, 'tbl_11': tbl_11, 'tbl_12': tbl_12, 'tbl_13': tbl_13, 'tbl_14': tbl_14, 'tbl_15': tbl_15, 'tbl_16': tbl_16, 'tbl_17': tbl_17, 'tbl_18': tbl_18, 'tbl_19': tbl_19, 'tbl_20': tbl_20, 'tbl_21': tbl_21, 'tbl_22': tbl_22, 'tbl_23': tbl_23, 'tbl_24': tbl_24, 'tbl_25': tbl_25, 'tbl_26': tbl_26, 'tbl_27': tbl_27, 'tbl_28': tbl_28, 'tbl_29': tbl_29, 'tbl_30': tbl_30, 'tbl_31': tbl_31, 'W_top1': W_top1, 'b_top1': b_top1, 'W_top2': W_top2, 'b_top2': b_top2, 'W_top3': W_top3, 'L0_rec_W0': _L0_rec_in['W0'], 'L0_rec_W1': _L0_rec_in['W1'], 'L0_rec_W2': _L0_rec_in['W2']}

def reference(dense_ctx, ids, tbl_0, tbl_1, tbl_2, tbl_3, tbl_4, tbl_5, tbl_6, tbl_7, tbl_8, tbl_9, tbl_10, tbl_11, tbl_12, tbl_13, tbl_14, tbl_15, tbl_16, tbl_17, tbl_18, tbl_19, tbl_20, tbl_21, tbl_22, tbl_23, tbl_24, tbl_25, tbl_26, tbl_27, tbl_28, tbl_29, tbl_30, tbl_31, W_top1, b_top1, W_top2, b_top2, W_top3, L0_rec_W0, L0_rec_W1, L0_rec_W2):
    import jax
    import jax.numpy as jnp

    def _L0_rec_ref(embeddings, W0, W1, W2):
        import jax, jax.numpy as jnp
        import numpy as np
        B, M, D = (2048, 32, 16)
        LAYERS = [64, 64, 64]
        x0 = embeddings
        xk = x0
        outs = []
        for W in (W0, W1, W2):
            xk = jax.nn.relu(jnp.einsum('bmd,bhd,mhk->bkd', x0, xk, W))
            outs.append(jnp.sum(xk, axis=2))
        return jnp.concatenate(outs, axis=1)
    e = jnp.stack([tbl_0[ids[:, 0]], tbl_1[ids[:, 1]], tbl_2[ids[:, 2]], tbl_3[ids[:, 3]], tbl_4[ids[:, 4]], tbl_5[ids[:, 5]], tbl_6[ids[:, 6]], tbl_7[ids[:, 7]], tbl_8[ids[:, 8]], tbl_9[ids[:, 9]], tbl_10[ids[:, 10]], tbl_11[ids[:, 11]], tbl_12[ids[:, 12]], tbl_13[ids[:, 13]], tbl_14[ids[:, 14]], tbl_15[ids[:, 15]], tbl_16[ids[:, 16]], tbl_17[ids[:, 17]], tbl_18[ids[:, 18]], tbl_19[ids[:, 19]], tbl_20[ids[:, 20]], tbl_21[ids[:, 21]], tbl_22[ids[:, 22]], tbl_23[ids[:, 23]], tbl_24[ids[:, 24]], tbl_25[ids[:, 25]], tbl_26[ids[:, 26]], tbl_27[ids[:, 27]], tbl_28[ids[:, 28]], tbl_29[ids[:, 29]], tbl_30[ids[:, 30]], tbl_31[ids[:, 31]]], axis=1)
    z = _L0_rec_ref(e, L0_rec_W0, L0_rec_W1, L0_rec_W2)
    z = z.reshape(z.shape[0], -1)
    h = jnp.concatenate([z, dense_ctx], axis=1)
    h = jnp.maximum(h @ W_top1 + b_top1, 0.0)
    h = jnp.maximum(h @ W_top2 + b_top2, 0.0)
    y = h @ W_top3
    return y

_drawn_inputs = setup_inputs


def setup_inputs(seed=0):
    import zlib

    import numpy as np

    out = dict(_drawn_inputs(seed))
    spreads = {'b_top1': (0.0, 2.0), 'b_top2': (0.0, 0.8)}
    factors = {'tbl_0': 8.0,
     'tbl_1': 8.0,
     'tbl_2': 8.0,
     'tbl_3': 8.0,
     'tbl_4': 8.0,
     'tbl_5': 8.0,
     'tbl_6': 8.0,
     'tbl_7': 8.0,
     'tbl_8': 8.0,
     'tbl_9': 8.0,
     'tbl_10': 8.0,
     'tbl_11': 8.0,
     'tbl_12': 8.0,
     'tbl_13': 8.0,
     'tbl_14': 8.0,
     'tbl_15': 8.0,
     'tbl_16': 8.0,
     'tbl_17': 8.0,
     'tbl_18': 8.0,
     'tbl_19': 8.0,
     'tbl_20': 8.0,
     'tbl_21': 8.0,
     'tbl_22': 8.0,
     'tbl_23': 8.0,
     'tbl_24': 8.0,
     'tbl_25': 8.0,
     'tbl_26': 8.0,
     'tbl_27': 8.0,
     'tbl_28': 8.0,
     'tbl_29': 8.0,
     'tbl_30': 8.0,
     'tbl_31': 8.0,
     'L0_rec_W0': 3.779,
     'L0_rec_W1': 8.0,
     'L0_rec_W2': 8.0,
     'dense_ctx': 8.0}
    for name, (base, spread) in spreads.items():
        noise = np.random.default_rng([zlib.crc32(name.encode()), seed]).standard_normal(out[name].shape)
        drawn = base * np.exp(spread * noise) if base else spread * noise
        out[name] = jnp.asarray(drawn.astype(out[name].dtype))
    for name, factor in factors.items():
        out[name] = (out[name] * factor).astype(out[name].dtype)
    return out
```

```python
from contextlib import ExitStack

import concourse.bass as bass
from concourse import mybir

F32 = mybir.dt.float32
I32 = mybir.dt.int32
ALU = mybir.AluOpType
ACT = mybir.ActivationFunctionType
AX_X = mybir.AxisListType.X

P = 128
BATCH, FIELDS, DIM, HID = 512, 32, 16, 64
CHUNK = 32
N = CHUNK * DIM
PAIR = 2 * N
STREAMS = 2
GROUPS = BATCH // (2 * CHUNK * STREAMS)
PAIRS = GROUPS * STREAMS
MREP = 4
HROWS = P // MREP
TILES = FIELDS // MREP
HHALF = HID // HROWS
L0TILES = 5
QUART = 4
GATHERS = 2 * CHUNK // QUART
F_TOP1, F_TOP2 = 512, 256

PROLOGUE = [(0, 0), (0, 1)]
BODY = [(1, 0), (1, 1), (2, 0), (0, 0), (2, 1), (0, 1)]
LAST = [(1, 0), (1, 1), (2, 0), (2, 1)]
LOOPS = GROUPS - 1

ZRING = 3
PRING = 4
POOL_T = 2
GATHER_PLAN = {0: (0, 0, 10), 1: (0, 10, 16), 2: (1, 0, 16)}


def vector_units(layer):
    if layer == 0:
        return [(0, 0, 2), (0, 2, 2), (0, 4, 1)]
    return [(g, t, 2) for g in range(HHALF) for t in range(0, TILES - POOL_T, 2)]


def pool_units(layer):
    return [] if layer == 0 else [(g, t) for g in range(HHALF) for t in range(TILES - POOL_T, TILES)]


def tensor_order(layer):
    v, p = len(vector_units(layer)), len(pool_units(layer))
    if not p:
        return [("v", n) for n in range(v)]
    order, done = [], 0
    for n in range(v):
        while done < p and done * v < n * p:
            order.append(("p", done))
            done += 1
        if n == v - 1:
            order += [("p", m) for m in range(done, p)]
        order.append(("v", n))
    return order


SIZE = {
    "steps": lambda layer: 1,
    "vector": lambda layer: len(vector_units(layer)),
    "pool": lambda layer: len(pool_units(layer)),
    "relayed": lambda layer: 1 if layer == 0 else HHALF,
}


def total(what, steps):
    return sum(SIZE[what](layer) for layer, _ in steps)


class Section:

    def __init__(self, steps, it):
        self.steps, self.it = steps, it

    def before(self, what, k):
        if self.steps is PROLOGUE:
            return total(what, self.steps[:k])
        return total(what, PROLOGUE) + self.it * total(what, BODY) + total(what, self.steps[:k])

    def slot(self, what, k, ring):
        assert total(what, PROLOGUE) % ring == 0 and total(what, BODY) % ring == 0
        return total(what, self.steps[:k]) % ring

    def group(self, k):
        layer = self.steps[k][0]
        return 0 if self.steps is PROLOGUE else self.it + 1 if layer == 0 else self.it

    def relay_count(self, k):
        return 2 * self.group(k) + self.steps[k][0]


def table_rows(shapes):
    first, at = [], 0
    for rows in shapes:
        first.append(at)
        at += rows
    return first, at


def cin_dlrm(nc, table, ids, first_row, w0a, w0b, w1, w2, wt1, bt1, wt2, bt2, wt3, dense, out):
    with ExitStack() as ctx:
        def sb(name, shape, dt=F32):
            return ctx.enter_context(nc.sbuf_tensor(name, shape, dt))

        def ps(name, shape):
            return ctx.enter_context(nc.psum_tensor(name, shape, F32))

        def sem(name):
            return ctx.enter_context(nc.semaphore(name))

        fields_dram = [nc.dram_tensor(f"fields{s}", (2 * FIELDS, PAIR), F32).ap() for s in range(STREAMS)]

        ids_sb = sb("ids_sb", [P, PAIRS * GATHERS], I32)
        first_sb = sb("first_sb", [P, GATHERS], I32)
        index = [sb(f"index{s}", [P, GATHERS], I32) for s in range(STREAMS)]
        gathered = [sb(f"gathered{s}", [P, GATHERS, DIM]) for s in range(STREAMS)]
        own = [sb(f"own{s}", [P, PAIR]) for s in range(STREAMS)]
        rotated = [sb(f"rotated{s}", [P, L0TILES, PAIR]) for s in range(STREAMS)]
        fields = [sb(f"fields_sb{s}", [P, TILES, PAIR]) for s in range(STREAMS)]
        hidden = [sb(f"hidden{s}", [P, HHALF, PAIR]) for s in range(STREAMS)]
        relu_out = [sb(f"relu_out{n}", [P, N]) for n in range(2)]
        vz = sb("vz", [P, ZRING, 2, PAIR])
        pz = sb("pz", [P, PRING, PAIR])
        w0a_sb = sb("w0a_sb", [P, L0TILES * HID])
        w0b_sb = sb("w0b_sb", [P, L0TILES * HID])
        w_sb = [sb("w0_sb", [P, L0TILES, HID]),
                sb("w1_sb", [P, HHALF * TILES, HID]), sb("w2_sb", [P, HHALF * TILES, HID])]
        feats = [sb(f"feats{layer}", [P, PAIRS, CHUNK]) for layer in range(3)]
        dense_sb = sb("dense_sb", [P, PAIRS * CHUNK])
        wt1_sb = sb("wt1_sb", [P, 3, F_TOP1])
        wt1d_sb = sb("wt1d_sb", [P, F_TOP1])
        wt2_sb = sb("wt2_sb", [P, F_TOP1 // P, F_TOP2])
        wt3_sb = sb("wt3_sb", [P, F_TOP2 // P])
        bt1_sb = sb("bt1_sb", [P, F_TOP1 // P])
        bt2_sb = sb("bt2_sb", [P, F_TOP2 // P])
        top1 = vz[:, 0, :, :].rearrange("p a (m n) -> p (a m) n", n=BATCH)
        top2 = vz[:, 1, 0, :].rearrange("p (m n) -> p m n", n=BATCH)
        y_sb = vz[0:1, 2, 0, 0:BATCH]

        factor = [ps(f"factor{n}", [P, PAIR]) for n in range(2)]
        acc = ps("acc", [P, 2, N])
        spare = ps("spare", [P, 2, N])

        ids_in = sem("ids_in")
        index_ready = sem("index_ready")
        rows_in = [sem(f"rows_in{s}") for s in range(STREAMS)]
        scratch_in = [sem(f"scratch_in{s}") for s in range(STREAMS)]
        own_in = [sem(f"own_in{s}") for s in range(STREAMS)]
        rotated_in = [sem(f"rotated_in{s}") for s in range(STREAMS)]
        fields_in = [sem(f"fields_in{s}") for s in range(STREAMS)]
        w0_in, w0_ready, w1_in, w2_in = sem("w0_in"), sem("w0_ready"), sem("w1_in"), sem("w2_in")
        top_in = sem("top_in")
        factor_ready = sem("factor_ready")
        vz_ready, vz_used = sem("vz_ready"), sem("vz_used")
        pz_ready, pz_used = sem("pz_ready"), sem("pz_used")
        relu_done, sums_done = sem("relu_done"), sem("sums_done")
        relayed = [sem(f"relayed{s}") for s in range(STREAMS)]
        top1_ps, top1_done = sem("top1_ps"), sem("top1_done")
        top2_ps, top2_done = sem("top2_ps"), sem("top2_done")
        y_ps, y_done, out_done = sem("y_ps"), sem("y_done"), sem("out_done")

        def top1_banks(m):
            room = [factor[0][:, :].rearrange("p (a n) -> p a n", a=2),
                    factor[1][:, :].rearrange("p (a n) -> p a n", a=2), spare[:, :, :], acc[:, :, :]][m]
            return room[:, :, 0:BATCH // 2]

        block = ctx.enter_context(nc.Block())

        @block.sync
        def _(sp):
            sp.dma_start(ids_sb[:, :], ids).then_inc(ids_in, 16)
            sp.dma_start(first_sb[:, :], first_row).then_inc(ids_in, 16)
            sp.dma_start(w0a_sb[:, :], w0a).then_inc(w0_in, 16)
            sp.dma_start(w0b_sb[:, :], w0b).then_inc(w0_in, 16)
            sp.dma_start(w_sb[1][:, :, :], w1).then_inc(w1_in, 16)
            sp.dma_start(w_sb[2][:, :, :], w2).then_inc(w2_in, 16)

            def held(value, name):
                register = sp.alloc_register(f"sp_{name}")
                sp.reg_mov(register, value)
                return sp.snap(register)

            def counts(s, g, section):
                values = {"rows": 16 * GATHERS * (g + 1), "scratch": 32 * (g + 1)}
                if section is not None:
                    values["read"] = 16 * TILES * g
                    layer0 = Section(PROLOGUE, 0) if section is PROLOGUE else Section(BODY, g - 2)
                    values["rotated_used"] = layer0.before("vector", layer0.steps.index((0, s)) + 1)
                    layer2, k = Section(BODY, g - 1), BODY.index((2, s)) + 1
                    values["fields_used"] = layer2.before("vector", k)
                    values["fields_used_pool"] = layer2.before("pool", k)
                return {name: v if isinstance(v, int) else held(v, f"{name}{s}") for name, v in values.items()}

            def spread(s, value):
                sp.wait_ge(rows_in[s], value["rows"])
                if "read" in value:
                    sp.wait_ge(fields_in[s], value["read"])
                for half in (fields_dram[s][0:FIELDS, :], fields_dram[s][FIELDS:2 * FIELDS, :]):
                    sp.dma_start(half.rearrange("m (q x) -> (m q) x", q=QUART),
                                 gathered[s][:, :, :].rearrange("p b d -> p (b d)")).then_inc(scratch_in[s], 16)
                sp.wait_ge(scratch_in[s], value["scratch"])
                if "rotated_used" in value:
                    sp.wait_ge(vz_ready, value["rotated_used"])
                span = fields_dram[s]
                sp.dma_start(own[s][:, :],
                             span[0:FIELDS, None, :].broadcast_to([FIELDS, MREP, PAIR])).then_inc(own_in[s], 16)
                for t in range(L0TILES):
                    turn = bass.AP(span.tensor, span.offset + MREP * t * PAIR,
                                   [[PAIR, FIELDS], [PAIR, MREP], [1, PAIR]])
                    sp.dma_start(rotated[s][:, t, :], turn).then_inc(rotated_in[s], 16)
                if "fields_used" in value:
                    sp.wait_ge(vz_ready, value["fields_used"])
                    sp.wait_ge(pz_ready, value["fields_used_pool"])
                for t in range(TILES):
                    each = bass.AP(span.tensor, span.offset + MREP * t * PAIR,
                                   [[0, HROWS], [PAIR, MREP], [1, PAIR]])
                    sp.dma_start(fields[s][:, t, :], each).then_inc(fields_in[s], 16)

            for s in range(STREAMS):
                spread(s, counts(s, 0, None))
            for half in range(2):
                rows = slice(half * HID, (half + 1) * HID)
                drows = slice(half * HID, half * HID + DIM)
                sp.dma_start(wt1_sb[rows, :, :],
                             wt1[0:3 * HID, :].rearrange("(l k) n -> k l n", k=HID)).then_inc(top_in, 16)
                sp.dma_start(wt1d_sb[drows, :], wt1[3 * HID:3 * HID + DIM, :]).then_inc(top_in, 16)
                sp.dma_start(dense_sb[drows, :], dense[half, :, :]).then_inc(top_in, 16)
            sp.dma_start(wt2_sb[:, :, :], wt2.rearrange("(m p) n -> p m n", p=P)).then_inc(top_in, 16)
            sp.dma_start(wt3_sb[:, :], wt3).then_inc(top_in, 16)
            sp.dma_start(bt1_sb[:, :], bt1).then_inc(top_in, 16)
            sp.dma_start(bt2_sb[:, :], bt2).then_inc(top_in, 16)

            for s in range(STREAMS):
                spread(s, counts(s, 1, PROLOGUE))
            with sp.Fori(2, GROUPS) as g:
                values = [counts(s, g, BODY) for s in range(STREAMS)]
                for s in range(STREAMS):
                    spread(s, values[s])

        @block.gpsimd
        def _(pool):
            def start_gathers(s, g):
                pair = STREAMS * g + s
                nc.gpsimd.tensor_tensor(index[s][:, :], ids_sb[:, bass.ds(pair * GATHERS, GATHERS)],
                                        first_sb[:, :], ALU.add).then_inc(index_ready, 1)
                pool.wait_ge(index_ready, pair + 1)

            def gather(s, i):
                nc.gpsimd.indirect_dma_start(
                    gathered[s][:, i, :], None, table,
                    bass.IndirectOffsetOnAxis(ap=index[s][:, i:i + 1], axis=0)).then_inc(rows_in[s], 16)

            def products(section, k, plan):
                layer, s = section.steps[k]
                n0, slot0 = section.before("pool", k), section.slot("pool", k, PRING)
                units = pool_units(layer)
                if units:
                    pool.wait_ge(relayed[s], 64 * section.relay_count(k))
                    if layer == 1:
                        pool.wait_ge(fields_in[s], 16 * TILES * (section.group(k) + 1))
                gs, i0, i1 = plan if plan else (0, 0, 0)
                if plan and i0 == 0:
                    pool.wait_ge(scratch_in[gs], 32 * (section.it + 1))
                    start_gathers(gs, section.it + 1)
                steps = max(len(units), 1)
                for u in range(steps):
                    if u < len(units):
                        g, t = units[u]
                        pool.wait_ge(pz_used, n0 + u + 1)
                        slot = (slot0 + u) % PRING
                        nc.gpsimd.tensor_tensor(pz[:, slot, :], fields[s][:, t, :], hidden[s][:, g, :],
                                                ALU.mult).then_inc(pz_ready, 1)
                    for i in range(i0 + (i1 - i0) * u // steps, i0 + (i1 - i0) * (u + 1) // steps):
                        gather(gs, i)

            pool.wait_ge(ids_in, 32)
            for s in range(STREAMS):
                start_gathers(s, 0)
                for i in range(GATHERS):
                    gather(s, i)
            with pool.Fori(0, LOOPS) as it:
                section = Section(BODY, it)
                for k in range(len(BODY)):
                    products(section, k, GATHER_PLAN.get(k))
            section = Section(LAST, LOOPS)
            for k in range(len(LAST)):
                products(section, k, None)

        @block.vector
        def _(dve):
            dve.wait_ge(w0_in, 32)
            nc.vector.tensor_tensor(w_sb[0][:, :, :].rearrange("p t k -> p (t k)"), w0a_sb[:, :], w0b_sb[:, :],
                                    ALU.add).then_inc(w0_ready, 1)

            def products(section, k):
                layer, s = section.steps[k]
                n0, slot0 = section.before("vector", k), section.slot("vector", k, ZRING)
                f0, fslot0 = section.before("relayed", k), section.slot("relayed", k, 2)
                if layer == 0:
                    dve.wait_ge(rotated_in[s], 16 * L0TILES * (section.group(k) + 1))
                elif layer == 1:
                    dve.wait_ge(fields_in[s], 16 * TILES * (section.group(k) + 1))
                at = -1
                for u, (g, t, nt) in enumerate(vector_units(layer)):
                    if g != at:
                        dve.wait_ge(factor_ready, f0 + g + 1)
                        at = g
                    if section.steps is not PROLOGUE or n0 + u >= ZRING:
                        dve.wait_ge(vz_used, n0 + u - ZRING + 1)
                    slot, fslot = (slot0 + u) % ZRING, (fslot0 + g) % 2
                    src = rotated[s] if layer == 0 else fields[s]
                    nc.vector.tensor_tensor(vz[:, slot, 0:nt, :], src[:, t:t + nt, :],
                                            factor[fslot][:, None, :].broadcast_to([P, nt, PAIR]),
                                            ALU.mult).then_inc(vz_ready, 1)

            def dim_sums(layer, s, g, n, slot):
                dve.wait_ge(relu_done, n + 1)
                nc.vector.tensor_reduce(feats[layer][:, bass.ds(STREAMS * g + s, 1), :],
                                        relu_out[slot][:, :].rearrange("p (a b d) -> p a b d", a=1, d=DIM),
                                        op=ALU.add, axis=AX_X).then_inc(sums_done, 1)

            def sums_of(section, k):
                layer, s = section.steps[k]
                dim_sums(layer, s, section.group(k), section.before("steps", k), k % 2)

            def sums_before(section):
                dim_sums(0, 1, section.it, section.before("steps", 0) - 1, 1)

            first = Section(PROLOGUE, 0)
            products(first, 0)
            products(first, 1)
            sums_of(first, 0)
            with dve.Fori(0, LOOPS) as it:
                section = Section(BODY, it)
                for k in range(len(BODY)):
                    products(section, k)
                    if k:
                        sums_of(section, k - 1)
                    else:
                        sums_before(section)
            section = Section(LAST, LOOPS)
            for k in range(len(LAST)):
                products(section, k)
                if k:
                    sums_of(section, k - 1)
                else:
                    sums_before(section)
            sums_of(section, len(LAST) - 1)

        @block.scalar
        def _(act):
            def put_factor(section, k):
                layer, s = section.steps[k]
                f0, fslot0 = section.before("relayed", k), section.slot("relayed", k, 2)
                for g in range(SIZE["relayed"](layer)):
                    if section.steps is not PROLOGUE:
                        act.wait_ge(vz_ready, slot_free(section, k, g))
                    if layer == 0:
                        act.wait_ge(own_in[s], 16 * (section.group(k) + 1))
                        src = own[s][:, :]
                    else:
                        act.wait_ge(relayed[s], 64 * section.relay_count(k))
                        src = hidden[s][:, g, :]
                    nc.scalar.activation(factor[(fslot0 + g) % 2][:, :], src, ACT.Copy).then_inc(factor_ready, 1)

            def slot_free(section, k, g):
                start = section.before("vector", k)
                if g == 1:
                    return start
                layer = section.steps[k - 1][0] if k else PROLOGUE[-1][0]
                halves = [h for h, _, _ in vector_units(layer)]
                return start - (halves.count(1) if 1 in halves else len(halves))

            def relu(section, k):
                layer, s = section.steps[k]
                n, slot = section.before("steps", k), k % 2
                act.wait_ge(vz_used, section.before("vector", k + 1))
                if section.steps is not PROLOGUE:
                    act.wait_ge(sums_done, n - 1)
                nc.scalar.activation(relu_out[slot][:, :], acc[:, slot, :], ACT.Relu).then_inc(relu_done, 1)
                if layer < 2:
                    act.wait_ge(relu_done, n + 1)
                    for g in range(HHALF):
                        for ab in range(2):
                            row = ab * HID + g * HROWS
                            act.dma_start(hidden[s][:, g, ab * N:(ab + 1) * N],
                                          relu_out[slot][row:row + HROWS, None, :]
                                          .broadcast_to([HROWS, MREP, N])).then_inc(relayed[s], 16)

            first = Section(PROLOGUE, 0)
            put_factor(first, 0)
            put_factor(first, 1)
            relu(first, 0)
            put_factor(Section(BODY, 0), 0)
            relu(first, 1)
            with act.Fori(0, LOOPS) as it:
                section = Section(BODY, it)
                for k in range(len(BODY)):
                    if k + 1 < len(BODY):
                        put_factor(section, k + 1)
                    else:
                        put_factor(Section(BODY, it + 1), 0)
                    relu(section, k)
            section = Section(LAST, LOOPS)
            for k in range(len(LAST)):
                if k + 1 < len(LAST):
                    put_factor(section, k + 1)
                relu(section, k)

            act.wait_ge(top_in, 160)
            for m in range(F_TOP1 // P):
                act.wait_ge(top1_ps, m + 1)
                nc.scalar.activation(top1[:, m, :].rearrange("p (a n) -> p a n", a=2), top1_banks(m),
                                     ACT.Relu, bias=bt1_sb[:, m:m + 1]).then_inc(top1_done, 1)
            for m in range(F_TOP2 // P):
                act.wait_ge(top2_ps, m + 1)
                nc.scalar.activation(top2[:, m, :], factor[0][:, m * N:(m + 1) * N], ACT.Relu,
                                     bias=bt2_sb[:, m:m + 1]).then_inc(top2_done, 1)
            act.wait_ge(y_ps, 1)
            nc.scalar.activation(y_sb, factor[1][0:1, 0:BATCH], ACT.Copy).then_inc(y_done, 1)
            act.wait_ge(y_done, 1)
            for ab in range(2):
                act.dma_start(out.rearrange("(c a j) o -> o a c j", a=2, j=CHUNK)[:, ab, :, :],
                              y_sb[:, ab * (BATCH // 2):(ab + 1) * (BATCH // 2)]
                              .rearrange("o (c j) -> o c j", j=CHUNK)).then_inc(out_done, 16)
            act.wait_ge(out_done, 32)

        @block.tensor
        def _(pe):
            pe.sem_inc(pz_used, PRING)

            def contract(section, k):
                layer, s = section.steps[k]
                n = section.before("steps", k)
                v0, vslot0 = section.before("vector", k), section.slot("vector", k, ZRING)
                p0, pslot0 = section.before("pool", k), section.slot("pool", k, PRING)
                if section.steps is not PROLOGUE:
                    pe.wait_ge(relu_done, n - 1)
                order = tensor_order(layer)
                for at, (who, u) in enumerate(order):
                    if who == "v":
                        g, t, nt = vector_units(layer)[u]
                        pe.wait_ge(vz_ready, v0 + u + 1)
                        slot = (vslot0 + u) % ZRING
                        pieces = [(g * TILES + t + j, vz[:, slot, j, :]) for j in range(nt)]
                    else:
                        g, t = pool_units(layer)[u]
                        pe.wait_ge(pz_ready, p0 + u + 1)
                        pieces = [(g * TILES + t, pz[:, (pslot0 + u) % PRING, :])]
                    for j, (kt, z) in enumerate(pieces):
                        start = at == 0 and j == 0
                        stop = at == len(order) - 1 and j == len(pieces) - 1
                        for ab in range(2):
                            last = nc.tensor.matmul(acc[ab * HID:(ab + 1) * HID, k % 2, :],
                                                    w_sb[layer][:, kt, :], z[:, ab * N:(ab + 1) * N],
                                                    start=start, stop=stop)
                    last.then_inc(vz_used if who == "v" else pz_used, 1)

            pe.wait_ge(w0_ready, 1)
            first = Section(PROLOGUE, 0)
            contract(first, 0)
            contract(first, 1)
            pe.wait_ge(w1_in, 16)
            pe.wait_ge(w2_in, 16)
            with pe.Fori(0, LOOPS) as it:
                for k in range(len(BODY)):
                    contract(Section(BODY, it), k)
            for k in range(len(LAST)):
                contract(Section(LAST, LOOPS), k)

            pe.wait_ge(top_in, 160)
            pe.wait_ge(relu_done, total("steps", PROLOGUE) + LOOPS * len(BODY) + len(LAST))
            pe.wait_ge(sums_done, total("steps", PROLOGUE) + LOOPS * len(BODY) + len(LAST))
            for m in range(F_TOP1 // P):
                cols = slice(m * P, (m + 1) * P)
                for piece in range(4):
                    for ab in range(2):
                        rows = slice(ab * HID, ab * HID + (HID if piece < 3 else DIM))
                        w = wt1_sb[rows, piece, cols] if piece < 3 else wt1d_sb[rows, cols]
                        x = feats[piece][rows, :, :].rearrange("p a b -> p (a b)") if piece < 3 else dense_sb[rows, :]
                        last = nc.tensor.matmul(top1_banks(m)[:, ab, :], w, x, start=piece == 0, stop=piece == 3)
                last.then_inc(top1_ps, 1)
            for m in range(F_TOP2 // P):
                for j in range(F_TOP1 // P):
                    if m == 0:
                        pe.wait_ge(top1_done, j + 1)
                    last = nc.tensor.matmul(factor[0][:, m * N:(m + 1) * N], wt2_sb[:, j, m * P:(m + 1) * P],
                                            top1[:, j, :], start=j == 0, stop=j == F_TOP1 // P - 1)
                last.then_inc(top2_ps, 1)
            for m in range(F_TOP2 // P):
                pe.wait_ge(top2_done, m + 1)
                last = nc.tensor.matmul(factor[1][0:1, 0:BATCH], wt3_sb[:, m:m + 1], top2[:, m, :],
                                        start=m == 0, stop=m == F_TOP2 // P - 1)
            last.then_inc(y_ps, 1)


def kernel(**inputs):
    import numpy as np
    import concourse.bacc as bacc
    from concourse.bass_utils import run_bass_kernel_spmd

    tables = [inputs[f"tbl_{f}"] for f in range(FIELDS)]
    first, _ = table_rows([t.shape[0] for t in tables])
    table = np.concatenate([np.asarray(t) for t in tables], axis=0)
    ids = np.asarray(inputs["ids"]).reshape(PAIRS, QUART, GATHERS, FIELDS).transpose(3, 1, 0, 2)
    ids = np.ascontiguousarray(ids.reshape(P, PAIRS * GATHERS))
    first_row = np.repeat(np.repeat(np.array(first, np.int32), QUART)[:, None], GATHERS, axis=1)
    w0 = np.asarray(inputs["L0_rec_W0"])
    w0a = np.zeros((FIELDS, MREP, L0TILES, HID), w0.dtype)
    w0b = np.zeros((FIELDS, MREP, L0TILES, HID), w0.dtype)
    h = np.arange(FIELDS)
    for r in range(FIELDS // 2 + 1):
        w0a[:, r % MREP, r // MREP] = w0[h, (h + r) % FIELDS]
        if 0 < r < FIELDS // 2:
            w0b[:, r % MREP, r // MREP] = w0[(h + r) % FIELDS, h]

    def upper(w):
        w = np.asarray(w).reshape(TILES, MREP, HHALF, HROWS, HID).transpose(3, 1, 2, 0, 4)
        return np.ascontiguousarray(w.reshape(P, HHALF * TILES, HID))

    def columns(v, tiles):
        return np.ascontiguousarray(np.asarray(v).reshape(tiles, P).T)

    dense = np.asarray(inputs["dense_ctx"]).reshape(PAIRS, 2, CHUNK, DIM).transpose(1, 3, 0, 2)
    arrays = {
        "table": table, "ids": ids, "first_row": first_row,
        "w0a": w0a.reshape(P, -1), "w0b": w0b.reshape(P, -1),
        "w1": upper(inputs["L0_rec_W1"]), "w2": upper(inputs["L0_rec_W2"]),
        "wt1": np.asarray(inputs["W_top1"]), "bt1": columns(inputs["b_top1"], F_TOP1 // P),
        "wt2": np.asarray(inputs["W_top2"]), "bt2": columns(inputs["b_top2"], F_TOP2 // P),
        "wt3": columns(inputs["W_top3"], F_TOP2 // P),
        "dense": np.ascontiguousarray(dense.reshape(2, DIM, PAIRS * CHUNK)),
    }
    nc = bacc.Bacc("TRN2", target_bir_lowering=False, num_devices=1)
    arrays = {f"in_{k}": np.ascontiguousarray(v) for k, v in arrays.items()}
    args = [nc.dram_tensor(k, v.shape, mybir.dt.from_np(v.dtype), kind="ExternalInput").ap()
            for k, v in arrays.items()]
    out = nc.dram_tensor("out_y", (BATCH, 1), F32, kind="ExternalOutput").ap()
    cin_dlrm(nc, *args, out)
    r = run_bass_kernel_spmd(nc, [arrays], core_ids=[0])
    return r.results[0]["out_y"]
```

```python
from contextlib import ExitStack

import concourse.bass as bass
from concourse import mybir

F32 = mybir.dt.float32
I32 = mybir.dt.int32
ALU = mybir.AluOpType
ACT = mybir.ActivationFunctionType
AX_X = mybir.AxisListType.X

P = 128
BATCH, FIELDS, DIM, HID = 512, 32, 16, 64
CHUNK = 32
N = CHUNK * DIM
PAIR = 2 * N
STREAMS = 2
GROUPS = BATCH // (2 * CHUNK * STREAMS)
PAIRS = GROUPS * STREAMS
MREP = 4
HROWS = P // MREP
TILES = FIELDS // MREP
HHALF = HID // HROWS
L0TILES = 5
QUART = 4
GATHERS = 2 * CHUNK // QUART
F_TOP1, F_TOP2 = 512, 256

PROLOGUE = [(0, 0), (0, 1), (1, 0), (1, 1), (2, 0)]
BODY = [(0, 0), (2, 1), (0, 1), (1, 0), (1, 1), (2, 0)]
END = [(2, 1)]
ALL_STEPS = len(PROLOGUE) + (GROUPS - 1) * len(BODY) + len(END)

ZRING = 3
PRING = 4
POOL_T = 2
FIELDS_ORDER = [6, 0, 1, 7, 2, 3, 4, 5]
EARLY_FIELDS = 2
PROLOGUE_GATHERS = {0: [(0, 0, 14)], 2: [(0, 14, 16), (1, 0, 4)], 3: [(1, 4, 10)], 4: [(1, 10, 16)]}
BODY_GATHERS = {1: [(0, 0, 12)], 3: [(0, 12, 16), (1, 0, 8)], 4: [(1, 8, 14)], 5: [(1, 14, 16)]}
IN_FLIGHT = 3


def vector_units(layer):
    if layer == 0:
        return [(0, 0, 2), (0, 2, 2), (0, 4, 1)]
    return [(g, t, 2) for g in range(HHALF) for t in range(0, TILES - POOL_T, 2)]


def pool_units(layer):
    return [] if layer == 0 else [(g, t) for g in range(HHALF) for t in range(TILES - POOL_T, TILES)]


def tensor_order(layer):
    v, p = len(vector_units(layer)), len(pool_units(layer))
    if not p:
        return [("v", n) for n in range(v)]
    order, done = [], 0
    for n in range(v):
        while done < p and done * v < n * p:
            order.append(("p", done))
            done += 1
        if n == v - 1:
            order += [("p", m) for m in range(done, p)]
        order.append(("v", n))
    return order


SIZE = {
    "steps": lambda layer: 1,
    "vector": lambda layer: len(vector_units(layer)),
    "pool": lambda layer: len(pool_units(layer)),
    "relayed": lambda layer: 1 if layer == 0 else HHALF,
}


def total(what, steps):
    return sum(SIZE[what](layer) for layer, _ in steps)


class Section:

    def __init__(self, steps, g):
        self.steps, self.g = steps, g

    def before(self, what, k):
        if self.steps is PROLOGUE:
            return total(what, self.steps[:k])
        return total(what, PROLOGUE) + (self.g - 1) * total(what, BODY) + total(what, self.steps[:k])

    def slot(self, what, k, ring):
        assert total(what, BODY) % ring == 0
        ahead = [] if self.steps is PROLOGUE else PROLOGUE
        return (total(what, ahead) + total(what, self.steps[:k])) % ring

    def group(self, k):
        if self.steps is PROLOGUE:
            return 0
        return self.g - 1 if self.steps[k] == (2, 1) else self.g

    def relay_count(self, k):
        return 2 * self.group(k) + self.steps[k][0]


def table_rows(shapes):
    first, at = [], 0
    for rows in shapes:
        first.append(at)
        at += rows
    return first, at


def cin_dlrm(nc, table, ids, first_row, w0a, w0b, w1, w2, wt1, bt1, wt2, bt2, wt3, dense, out):
    with ExitStack() as ctx:
        def sb(name, shape, dt=F32):
            return ctx.enter_context(nc.sbuf_tensor(name, shape, dt))

        def ps(name, shape):
            return ctx.enter_context(nc.psum_tensor(name, shape, F32))

        def sem(name):
            return ctx.enter_context(nc.semaphore(name))

        fields_dram = [nc.dram_tensor(f"fields{s}", (2 * FIELDS, PAIR), F32).ap() for s in range(STREAMS)]

        ids_sb = sb("ids_sb", [P, PAIRS * GATHERS], I32)
        first_sb = sb("first_sb", [P, GATHERS], I32)
        index = [sb(f"index{s}", [P, GATHERS], I32) for s in range(STREAMS)]
        gathered = [sb(f"gathered{s}", [P, GATHERS, DIM]) for s in range(STREAMS)]
        own = [sb(f"own{s}", [P, PAIR]) for s in range(STREAMS)]
        rotated = [sb(f"rotated{s}", [P, L0TILES, PAIR]) for s in range(STREAMS)]
        fields = [sb(f"fields_sb{s}", [P, TILES, PAIR]) for s in range(STREAMS)]
        hidden = [sb(f"hidden{s}", [P, HHALF, PAIR]) for s in range(STREAMS)]
        relu_out = [sb(f"relu_out{n}", [P, N]) for n in range(2)]
        vz = sb("vz", [P, ZRING, 2, PAIR])
        pz = sb("pz", [P, PRING, PAIR])
        w0a_sb = sb("w0a_sb", [P, L0TILES * HID])
        w0b_sb = sb("w0b_sb", [P, L0TILES * HID])
        w_sb = [sb("w0_sb", [P, L0TILES, HID]),
                sb("w1_sb", [P, HHALF * TILES, HID]), sb("w2_sb", [P, HHALF * TILES, HID])]
        feats = [sb(f"feats{layer}", [P, PAIRS, CHUNK]) for layer in range(3)]
        stack01 = sb("stack01", [P, BATCH])
        stack2 = sb("stack2", [P, BATCH])
        wt1_sb = sb("wt1_sb", [P, F_TOP1])
        wt1d_sb = sb("wt1d_sb", [P, F_TOP1])
        wt2_sb = sb("wt2_sb", [P, F_TOP1 // P, F_TOP2])
        wt3_sb = sb("wt3_sb", [P, F_TOP2 // P])
        bt1_sb = sb("bt1_sb", [P, F_TOP1 // P])
        bt2_sb = sb("bt2_sb", [P, F_TOP2 // P])
        top1 = vz[:, 0, :, :].rearrange("p a (m n) -> p (a m) n", n=BATCH)
        top2 = vz[:, 1, 0, :].rearrange("p (m n) -> p m n", n=BATCH)
        y_sb = vz[0:1, 2, 0, 0:BATCH]

        factor = [ps(f"factor{n}", [P, PAIR]) for n in range(2)]
        acc = ps("acc", [P, 2, N])
        spare = ps("spare", [P, 2, N])

        ids_in = sem("ids_in")
        index_ready = sem("index_ready")
        rows_in = [sem(f"rows_in{s}") for s in range(STREAMS)]
        scratch_in = [sem(f"scratch_in{s}") for s in range(STREAMS)]
        own_in = [sem(f"own_in{s}") for s in range(STREAMS)]
        rotated_in = [[sem(f"rotated_in{s}_{t}") for t in range(L0TILES)] for s in range(STREAMS)]
        fields_in = [[sem(f"fields_in{s}_{t}") for t in range(TILES)] for s in range(STREAMS)]
        w0_in, w0_ready, w1_in, w2_in = sem("w0_in"), sem("w0_ready"), sem("w1_in"), sem("w2_in")
        top_in, stack01_in, stack2_in = sem("top_in"), sem("stack01_in"), sem("stack2_in")
        factor_ready = sem("factor_ready")
        vz_ready, vz_used = sem("vz_ready"), sem("vz_used")
        pz_ready, pz_used = sem("pz_ready"), sem("pz_used")
        relu_done, sums_done = sem("relu_done"), sem("sums_done")
        relayed = [[sem(f"relayed{s}_{g}") for g in range(HHALF)] for s in range(STREAMS)]
        top1_ps, top1_done = sem("top1_ps"), sem("top1_done")
        top2_ps, top2_done = sem("top2_ps"), sem("top2_done")
        y_ps, y_done, out_done = sem("y_ps"), sem("y_done"), sem("out_done")

        def top1_bank(m):
            return factor[m // 2][:, (m % 2) * N:(m % 2 + 1) * N]

        block = ctx.enter_context(nc.Block())

        @block.sync
        def _(sp):
            sp.dma_start(ids_sb[:, :], ids).then_inc(ids_in, 16)
            sp.dma_start(first_sb[:, :], first_row).then_inc(ids_in, 16)
            sp.dma_start(w0a_sb[:, :], w0a).then_inc(w0_in, 16)
            sp.dma_start(w0b_sb[:, :], w0b).then_inc(w0_in, 16)
            sp.dma_start(w_sb[1][:, :, :], w1).then_inc(w1_in, 16)
            sp.dma_start(w_sb[2][:, :, :], w2).then_inc(w2_in, 16)

            sp.dma_start(wt1_sb[:, :], wt1[0:2 * HID, :]).then_inc(top_in, 16)
            sp.dma_start(wt1d_sb[0:HID + DIM, :], wt1[2 * HID:3 * HID + DIM, :]).then_inc(top_in, 16)
            sp.dma_start(stack2[HID:HID + DIM, :], dense).then_inc(top_in, 16)
            sp.dma_start(wt2_sb[:, :, :], wt2.rearrange("(m p) n -> p m n", p=P)).then_inc(top_in, 16)
            sp.dma_start(wt3_sb[:, :], wt3).then_inc(top_in, 16)
            sp.dma_start(bt1_sb[:, :], bt1).then_inc(top_in, 16)
            sp.dma_start(bt2_sb[:, :], bt2).then_inc(top_in, 16)

            def held(value, name):
                register = sp.alloc_register(f"sp_{name}")
                sp.reg_mov(register, value)
                return sp.snap(register)

            def named(values, name):
                return {k: v if isinstance(v, int) else held(v, f"{name}_{k}") for k, v in values.items()}

            def counts(s, g, last):
                values = {"rows": 16 * GATHERS * (g + 1), "scratch": 32 * (g + 1), "loaded": 16 * (g + 1)}
                if last is not None:
                    values["read"] = 16 * g
                    values["rotated_used"] = last.before("vector", last.steps.index((0, s)) + 1)
                return named(values, f"rows{s}")

            def field_counts(s, g):
                values = {"loaded": 16 * (g + 1)}
                if not isinstance(g, int) or g:
                    layer2, k = (Section(BODY, g - 1), len(BODY)) if s == 0 else (Section(BODY, g), 2)
                    values["fields_used"] = layer2.before("vector", k)
                    values["fields_used_pool"] = layer2.before("pool", k)
                return named(values, f"fields{s}")

            def to_scratch(s, value):
                sp.wait_ge(rows_in[s], value["rows"])
                if "read" in value:
                    for t in FIELDS_ORDER[-IN_FLIGHT:]:
                        sp.wait_ge(fields_in[s][t], value["read"])
                for half in (fields_dram[s][0:FIELDS, :], fields_dram[s][FIELDS:2 * FIELDS, :]):
                    sp.dma_start(half.rearrange("m (q x) -> (m q) x", q=QUART),
                                 gathered[s][:, :, :].rearrange("p b d -> p (b d)")).then_inc(scratch_in[s], 16)

            def spread_rotated(s, value):
                sp.wait_ge(scratch_in[s], value["scratch"])
                if "rotated_used" in value:
                    sp.wait_ge(vz_ready, value["rotated_used"])
                span = fields_dram[s]
                sp.dma_start(own[s][:, :],
                             span[0:FIELDS, None, :].broadcast_to([FIELDS, MREP, PAIR])).then_inc(own_in[s], 16)
                sent = [own_in[s]]
                for t in range(L0TILES):
                    turn = bass.AP(span.tensor, span.offset + MREP * t * PAIR,
                                   [[PAIR, FIELDS], [PAIR, MREP], [1, PAIR]])
                    if len(sent) >= IN_FLIGHT:
                        sp.wait_ge(sent[-IN_FLIGHT], value["loaded"])
                    sp.dma_start(rotated[s][:, t, :], turn).then_inc(rotated_in[s][t], 16)
                    sent.append(rotated_in[s][t])

            def spread(s, value):
                to_scratch(s, value)
                spread_rotated(s, value)

            def spread_fields(s, value, first=0, end=TILES):
                span = fields_dram[s]
                if first == 0 and "fields_used" in value:
                    sp.wait_ge(vz_ready, value["fields_used"])
                    sp.wait_ge(pz_ready, value["fields_used_pool"])
                for n in range(first, end):
                    t = FIELDS_ORDER[n]
                    each = bass.AP(span.tensor, span.offset + MREP * t * PAIR,
                                   [[0, HROWS], [PAIR, MREP], [1, PAIR]])
                    if n >= IN_FLIGHT:
                        sp.wait_ge(fields_in[s][FIELDS_ORDER[n - IN_FLIGHT]], value["loaded"])
                    sp.dma_start(fields[s][:, t, :], each).then_inc(fields_in[s][t], 16)

            spread(0, counts(0, 0, None))
            spread_fields(0, field_counts(0, 0), 0, EARLY_FIELDS)
            spread(1, counts(1, 0, None))
            spread_fields(0, field_counts(0, 0), EARLY_FIELDS)
            spread_fields(1, field_counts(1, 0))
            for s in range(STREAMS):
                spread(s, counts(s, 1, Section(PROLOGUE, 0)))
            with sp.Fori(1, GROUPS - 1) as g:
                now = [field_counts(s, g) for s in range(STREAMS)]
                after = [counts(s, g + 1, Section(BODY, g)) for s in range(STREAMS)]
                for s in range(STREAMS):
                    spread_fields(s, now[s])
                for s in range(STREAMS):
                    spread(s, after[s])
            for s in range(STREAMS):
                spread_fields(s, field_counts(s, GROUPS - 1))

            half_cols = BATCH // 2
            for layer in range(2):
                k = BODY.index((layer, 1))
                sp.wait_ge(sums_done, Section(BODY, GROUPS - 1).before("steps", k + 1))
                for ab in range(2):
                    sp.dma_start(stack01[layer * HID:(layer + 1) * HID, ab * half_cols:(ab + 1) * half_cols],
                                 feats[layer][ab * HID:(ab + 1) * HID, :, :].rearrange("p c j -> p (c j)")) \
                      .then_inc(stack01_in, 16)
            sp.wait_ge(sums_done, ALL_STEPS)
            for ab in range(2):
                sp.dma_start(stack2[0:HID, ab * half_cols:(ab + 1) * half_cols],
                             feats[2][ab * HID:(ab + 1) * HID, :, :].rearrange("p c j -> p (c j)")) \
                  .then_inc(stack2_in, 16)

        @block.gpsimd
        def _(pool):
            def start_gathers(s, g):
                pair = STREAMS * g + s
                nc.gpsimd.tensor_tensor(index[s][:, :], ids_sb[:, bass.ds(pair * GATHERS, GATHERS)],
                                        first_sb[:, :], ALU.add).then_inc(index_ready, 1)
                pool.wait_ge(index_ready, pair + 1)

            def gather(s, i):
                nc.gpsimd.indirect_dma_start(
                    gathered[s][:, i, :], None, table,
                    bass.IndirectOffsetOnAxis(ap=index[s][:, i:i + 1], axis=0)).then_inc(rows_in[s], 16)

            def products(section, k, plan):
                layer, s = section.steps[k]
                n0, slot0 = section.before("pool", k), section.slot("pool", k, PRING)
                units = pool_units(layer)
                for gs, i0, _ in plan:
                    if i0 == 0:
                        g = 1 if section.steps is PROLOGUE else section.g + 1
                        pool.wait_ge(scratch_in[gs], 32 * g)
                        start_gathers(gs, g)
                todo = [(gs, i) for gs, i0, i1 in plan for i in range(i0, i1)]
                for u, (g, t) in enumerate(units):
                    if layer == 1 and g == 0:
                        pool.wait_ge(fields_in[s][t], 16 * (section.group(k) + 1))
                    if t == TILES - POOL_T:
                        pool.wait_ge(relayed[s][g], 32 * section.relay_count(k))
                    pool.wait_ge(pz_used, n0 + u + 1)
                    slot = (slot0 + u) % PRING
                    nc.gpsimd.tensor_tensor(pz[:, slot, :], fields[s][:, t, :], hidden[s][:, g, :],
                                            ALU.mult).then_inc(pz_ready, 1)
                for gs, i in todo:
                    gather(gs, i)

            pool.wait_ge(ids_in, 32)
            for s in range(STREAMS):
                start_gathers(s, 0)
                for i in range(GATHERS):
                    gather(s, i)
            for k in range(len(PROLOGUE)):
                products(Section(PROLOGUE, 0), k, PROLOGUE_GATHERS.get(k, []))
            with pool.Fori(1, GROUPS - 1) as g:
                for k in range(len(BODY)):
                    products(Section(BODY, g), k, BODY_GATHERS.get(k, []))
            for k in range(len(BODY)):
                products(Section(BODY, GROUPS - 1), k, [])
            products(Section(END, GROUPS), 0, [])

        @block.vector
        def _(dve):
            dve.wait_ge(w0_in, 32)
            nc.vector.tensor_tensor(w_sb[0][:, :, :].rearrange("p t k -> p (t k)"), w0a_sb[:, :], w0b_sb[:, :],
                                    ALU.add).then_inc(w0_ready, 1)

            def products(section, k):
                layer, s = section.steps[k]
                n0, slot0 = section.before("vector", k), section.slot("vector", k, ZRING)
                f0, fslot0 = section.before("relayed", k), section.slot("relayed", k, 2)
                at = -1
                for u, (g, t, nt) in enumerate(vector_units(layer)):
                    if g != at:
                        dve.wait_ge(factor_ready, f0 + g + 1)
                        at = g
                    arrived = [rotated_in, fields_in, fields_in][layer][s]
                    for tile in range(t, t + nt):
                        if layer < 2 and g == 0:
                            dve.wait_ge(arrived[tile], 16 * (section.group(k) + 1))
                    if section.steps is not PROLOGUE or n0 + u >= ZRING:
                        dve.wait_ge(vz_used, n0 + u - ZRING + 1)
                    slot, fslot = (slot0 + u) % ZRING, (fslot0 + g) % 2
                    src = rotated[s] if layer == 0 else fields[s]
                    nc.vector.tensor_tensor(vz[:, slot, 0:nt, :], src[:, t:t + nt, :],
                                            factor[fslot][:, None, :].broadcast_to([P, nt, PAIR]),
                                            ALU.mult).then_inc(vz_ready, 1)

            def dim_sums(layer, s, g, n, slot):
                dve.wait_ge(relu_done, n + 1)
                nc.vector.tensor_reduce(feats[layer][:, bass.ds(STREAMS * g + s, 1), :],
                                        relu_out[slot][:, :].rearrange("p (a b d) -> p a b d", a=1, d=DIM),
                                        op=ALU.add, axis=AX_X).then_inc(sums_done, 1)

            def sums_of(section, k):
                layer, s = section.steps[k]
                dim_sums(layer, s, section.group(k), section.before("steps", k), section.slot("steps", k, 2))

            def sums_before(section):
                n, slot = section.before("steps", 0) - 1, (section.slot("steps", 0, 2) + 1) % 2
                dim_sums(2, 0, section.g - 1, n, slot)

            for k in range(len(PROLOGUE)):
                products(Section(PROLOGUE, 0), k)
                if k:
                    sums_of(Section(PROLOGUE, 0), k - 1)
            with dve.Fori(1, GROUPS) as g:
                for k in range(len(BODY)):
                    products(Section(BODY, g), k)
                    if k:
                        sums_of(Section(BODY, g), k - 1)
                    else:
                        sums_before(Section(BODY, g))
            products(Section(END, GROUPS), 0)
            sums_before(Section(END, GROUPS))
            sums_of(Section(END, GROUPS), 0)

        @block.scalar
        def _(act):
            def put_factor(section, k):
                layer, s = section.steps[k]
                f0, fslot0 = section.before("relayed", k), section.slot("relayed", k, 2)
                for g in range(SIZE["relayed"](layer)):
                    if section.steps is not PROLOGUE or f0 + g >= 2:
                        act.wait_ge(vz_ready, slot_free(section, k, g))
                    if layer == 0:
                        act.wait_ge(own_in[s], 16 * (section.group(k) + 1))
                        src = own[s][:, :]
                    else:
                        act.wait_ge(relayed[s][g], 32 * section.relay_count(k))
                        src = hidden[s][:, g, :]
                    nc.scalar.activation(factor[(fslot0 + g) % 2][:, :], src, ACT.Copy).then_inc(factor_ready, 1)

            def slot_free(section, k, g):
                start = section.before("vector", k)
                if g == 1:
                    return start
                layer = section.steps[k - 1][0] if k else 2
                halves = [h for h, _, _ in vector_units(layer)]
                return start - (halves.count(1) if 1 in halves else len(halves))

            def relu(section, k):
                layer, s = section.steps[k]
                n, slot = section.before("steps", k), section.slot("steps", k, 2)
                act.wait_ge(vz_used, section.before("vector", k + 1))
                if section.steps is not PROLOGUE or n >= 2:
                    act.wait_ge(sums_done, n - 1)
                nc.scalar.activation(relu_out[slot][:, :], acc[:, slot, :], ACT.Relu).then_inc(relu_done, 1)
                if layer < 2:
                    act.wait_ge(relu_done, n + 1)
                    for g in range(HHALF):
                        for ab in range(2):
                            row = ab * HID + g * HROWS
                            act.dma_start(hidden[s][:, g, ab * N:(ab + 1) * N],
                                          relu_out[slot][row:row + HROWS, None, :]
                                          .broadcast_to([HROWS, MREP, N])).then_inc(relayed[s][g], 16)

            put_factor(Section(PROLOGUE, 0), 0)
            for k in range(len(PROLOGUE)):
                section = Section(PROLOGUE, 0)
                after = (section, k + 1) if k + 1 < len(PROLOGUE) else (Section(BODY, 1), 0)
                relay_first = k == 0
                if not relay_first:
                    put_factor(*after)
                relu(section, k)
                if relay_first:
                    put_factor(*after)
            with act.Fori(1, GROUPS - 1) as g:
                for k in range(len(BODY)):
                    if k + 1 < len(BODY):
                        put_factor(Section(BODY, g), k + 1)
                    else:
                        put_factor(Section(BODY, g + 1), 0)
                    relu(Section(BODY, g), k)
            for k in range(len(BODY)):
                if k + 1 < len(BODY):
                    put_factor(Section(BODY, GROUPS - 1), k + 1)
                else:
                    put_factor(Section(END, GROUPS), 0)
                relu(Section(BODY, GROUPS - 1), k)
            relu(Section(END, GROUPS), 0)

            act.wait_ge(top_in, 112)
            for m in range(F_TOP1 // P):
                act.wait_ge(top1_ps, m + 1)
                nc.scalar.activation(top1[:, m, :], top1_bank(m),
                                     ACT.Relu, bias=bt1_sb[:, m:m + 1]).then_inc(top1_done, 1)
            for m in range(F_TOP2 // P):
                act.wait_ge(top2_ps, m + 1)
                nc.scalar.activation(top2[:, m, :], spare[:, m, :], ACT.Relu,
                                     bias=bt2_sb[:, m:m + 1]).then_inc(top2_done, 1)
            act.wait_ge(y_ps, 1)
            nc.scalar.activation(y_sb, acc[0:1, 0, :], ACT.Copy).then_inc(y_done, 1)
            act.wait_ge(y_done, 1)
            for ab in range(2):
                act.dma_start(out.rearrange("(c a j) o -> o a c j", a=2, j=CHUNK)[:, ab, :, :],
                              y_sb[:, ab * (BATCH // 2):(ab + 1) * (BATCH // 2)]
                              .rearrange("o (c j) -> o c j", j=CHUNK)).then_inc(out_done, 16)
            act.wait_ge(out_done, 32)

        @block.tensor
        def _(pe):
            pe.sem_inc(pz_used, PRING)

            def contract(section, k):
                layer, s = section.steps[k]
                n = section.before("steps", k)
                v0, vslot0 = section.before("vector", k), section.slot("vector", k, ZRING)
                p0, pslot0 = section.before("pool", k), section.slot("pool", k, PRING)
                bank = section.slot("steps", k, 2)
                if section.steps is not PROLOGUE or n >= 2:
                    pe.wait_ge(relu_done, n - 1)
                order = tensor_order(layer)
                for at, (who, u) in enumerate(order):
                    if who == "v":
                        g, t, nt = vector_units(layer)[u]
                        pe.wait_ge(vz_ready, v0 + u + 1)
                        slot = (vslot0 + u) % ZRING
                        pieces = [(g * TILES + t + j, vz[:, slot, j, :]) for j in range(nt)]
                    else:
                        g, t = pool_units(layer)[u]
                        pe.wait_ge(pz_ready, p0 + u + 1)
                        pieces = [(g * TILES + t, pz[:, (pslot0 + u) % PRING, :])]
                    for j, (kt, z) in enumerate(pieces):
                        start = at == 0 and j == 0
                        stop = at == len(order) - 1 and j == len(pieces) - 1
                        for ab in range(2):
                            last = nc.tensor.matmul(acc[ab * HID:(ab + 1) * HID, bank, :],
                                                    w_sb[layer][:, kt, :], z[:, ab * N:(ab + 1) * N],
                                                    start=start, stop=stop)
                    last.then_inc(vz_used if who == "v" else pz_used, 1)

            pe.wait_ge(w0_ready, 1)
            contract(Section(PROLOGUE, 0), 0)
            pe.wait_ge(w1_in, 16)
            pe.wait_ge(w2_in, 16)
            for k in range(1, len(PROLOGUE)):
                contract(Section(PROLOGUE, 0), k)
            with pe.Fori(1, GROUPS) as g:
                for k in range(len(BODY)):
                    contract(Section(BODY, g), k)
            contract(Section(END, GROUPS), 0)

            pe.wait_ge(top_in, 112)
            pe.wait_ge(stack01_in, 64)
            pe.wait_ge(vz_ready, Section(END, GROUPS).before("vector", 1))
            for m in range(F_TOP1 // P):
                nc.tensor.matmul(top1_bank(m), wt1_sb[:, m * P:(m + 1) * P], stack01[:, :], start=True, stop=False)
            pe.wait_ge(stack2_in, 32)
            for m in range(F_TOP1 // P):
                nc.tensor.matmul(top1_bank(m), wt1d_sb[0:HID + DIM, m * P:(m + 1) * P], stack2[0:HID + DIM, :],
                                 start=False, stop=True).then_inc(top1_ps, 1)
            for m in range(F_TOP2 // P):
                for j in range(F_TOP1 // P):
                    if m == 0:
                        pe.wait_ge(top1_done, j + 1)
                    last = nc.tensor.matmul(spare[:, m, :], wt2_sb[:, j, m * P:(m + 1) * P],
                                            top1[:, j, :], start=j == 0, stop=j == F_TOP1 // P - 1)
                last.then_inc(top2_ps, 1)
            for m in range(F_TOP2 // P):
                pe.wait_ge(top2_done, m + 1)
                last = nc.tensor.matmul(acc[0:1, 0, :], wt3_sb[:, m:m + 1], top2[:, m, :],
                                        start=m == 0, stop=m == F_TOP2 // P - 1)
            last.then_inc(y_ps, 1)


def kernel(**inputs):
    import numpy as np
    import concourse.bacc as bacc
    from concourse.bass_utils import run_bass_kernel_spmd

    tables = [inputs[f"tbl_{f}"] for f in range(FIELDS)]
    first, _ = table_rows([t.shape[0] for t in tables])
    table = np.concatenate([np.asarray(t) for t in tables], axis=0)
    ids = np.asarray(inputs["ids"]).reshape(PAIRS, QUART, GATHERS, FIELDS).transpose(3, 1, 0, 2)
    ids = np.ascontiguousarray(ids.reshape(P, PAIRS * GATHERS))
    first_row = np.repeat(np.repeat(np.array(first, np.int32), QUART)[:, None], GATHERS, axis=1)
    w0 = np.asarray(inputs["L0_rec_W0"])
    w0a = np.zeros((FIELDS, MREP, L0TILES, HID), w0.dtype)
    w0b = np.zeros((FIELDS, MREP, L0TILES, HID), w0.dtype)
    h = np.arange(FIELDS)
    for r in range(FIELDS // 2 + 1):
        w0a[:, r % MREP, r // MREP] = w0[h, (h + r) % FIELDS]
        if 0 < r < FIELDS // 2:
            w0b[:, r % MREP, r // MREP] = w0[(h + r) % FIELDS, h]

    def upper(w):
        w = np.asarray(w).reshape(TILES, MREP, HHALF, HROWS, HID).transpose(3, 1, 2, 0, 4)
        return np.ascontiguousarray(w.reshape(P, HHALF * TILES, HID))

    def columns(v, tiles):
        return np.ascontiguousarray(np.asarray(v).reshape(tiles, P).T)

    dense = np.asarray(inputs["dense_ctx"]).reshape(PAIRS, 2, CHUNK, DIM).transpose(3, 1, 0, 2)
    arrays = {
        "table": table, "ids": ids, "first_row": first_row,
        "w0a": w0a.reshape(P, -1), "w0b": w0b.reshape(P, -1),
        "w1": upper(inputs["L0_rec_W1"]), "w2": upper(inputs["L0_rec_W2"]),
        "wt1": np.asarray(inputs["W_top1"]), "bt1": columns(inputs["b_top1"], F_TOP1 // P),
        "wt2": np.asarray(inputs["W_top2"]), "bt2": columns(inputs["b_top2"], F_TOP2 // P),
        "wt3": columns(inputs["W_top3"], F_TOP2 // P),
        "dense": np.ascontiguousarray(dense.reshape(DIM, BATCH)),
    }
    nc = bacc.Bacc("TRN2", target_bir_lowering=False, num_devices=1)
    arrays = {f"in_{k}": np.ascontiguousarray(v) for k, v in arrays.items()}
    args = [nc.dram_tensor(k, v.shape, mybir.dt.from_np(v.dtype), kind="ExternalInput").ap()
            for k, v in arrays.items()]
    out = nc.dram_tensor("out_y", (BATCH, 1), F32, kind="ExternalOutput").ap()
    cin_dlrm(nc, *args, out)
    r = run_bass_kernel_spmd(nc, [arrays], core_ids=[0])
    return r.results[0]["out_y"]
```

```python
from contextlib import ExitStack

import concourse.bass as bass
from concourse import mybir

F32 = mybir.dt.float32
I32 = mybir.dt.int32
ALU = mybir.AluOpType
ACT = mybir.ActivationFunctionType
AX_X = mybir.AxisListType.X

P = 128
BATCH, FIELDS, DIM, HID = 512, 32, 16, 64
CHUNK = 32
N = CHUNK * DIM
PAIR = 2 * N
STREAMS = 2
GROUPS = BATCH // (2 * CHUNK * STREAMS)
PAIRS = GROUPS * STREAMS
MREP = 4
HROWS = P // MREP
TILES = FIELDS // MREP
HHALF = HID // HROWS
L0TILES = FIELDS // 2 // MREP
OPPOSITE = L0TILES
QCOLS = PAIR // MREP
QUART = 4
GATHERS = 2 * CHUNK // QUART
F_TOP1, F_TOP2 = 512, 256

PROLOGUE = [(0, 0), (0, 1), (1, 0), (1, 1), (2, 0)]
BODY = [(0, 0), (2, 1), (0, 1), (1, 0), (1, 1), (2, 0)]
END = [(2, 1)]
BY_TILE_STEP = 2
BY_TILE_ORDER = [("v", 0), ("p", 0), ("v", 1), ("p", 1), ("v", 2), ("p", 2), ("v", 3), ("p", 3), ("v", 4), ("v", 5)]
FACTORS = {(0, 0): 0, (1, 0): 1, (2, 0): 0, (2, 1): 1, (3, 0): 2, (3, 1): 1, (4, 0): 0, (4, 1): 1}
ALL_STEPS = len(PROLOGUE) + (GROUPS - 1) * len(BODY) + len(END)

ZRING = 3
PRING = 4
POOL_T = 2
FIELDS_ORDER = [6, 0, 1, 7, 2, 3, 4, 5]
EARLY_FIELDS = 4
FIRST_EARLY = (2, 3)
PROLOGUE_GATHERS = {0: [(0, 0, 14)], 2: [(0, 14, 16), (1, 0, 5)], 3: [(1, 5, 12)], 4: [(1, 12, 16)]}
BODY_GATHERS = {1: [(0, 0, 12)], 3: [(0, 12, 16), (1, 0, 4)], 4: [(1, 4, 10)], 5: [(1, 10, 16)]}
IN_FLIGHT = 3


def vector_units(layer, by_tile=False):
    if layer == 0:
        return [(0, 0, 2), (0, 2, 2), (0, OPPOSITE, 1)]
    units = [(g, t, 2) for g in range(HHALF) for t in range(0, TILES - POOL_T, 2)]
    return sorted(units, key=lambda unit: unit[1]) if by_tile else units


def pool_units(layer, by_tile=False):
    if layer == 0:
        return []
    units = [(g, t) for g in range(HHALF) for t in range(TILES - POOL_T, TILES)]
    return sorted(units, key=lambda unit: unit[1]) if by_tile else units


def tensor_order(layer, by_tile=False):
    if by_tile:
        return BY_TILE_ORDER
    v, p = len(vector_units(layer)), len(pool_units(layer))
    if not p:
        return [("v", n) for n in range(v)]
    order, done = [], 0
    for n in range(v):
        while done < p and done * v < n * p:
            order.append(("p", done))
            done += 1
        if n == v - 1:
            order += [("p", m) for m in range(done, p)]
        order.append(("v", n))
    return order


SIZE = {
    "steps": lambda layer: 1,
    "vector": lambda layer: len(vector_units(layer)),
    "pool": lambda layer: len(pool_units(layer)),
    "relayed": lambda layer: 1 if layer == 0 else HHALF,
}


def total(what, steps):
    return sum(SIZE[what](layer) for layer, _ in steps)


class Section:

    def __init__(self, steps, g):
        self.steps, self.g = steps, g

    def before(self, what, k):
        if self.steps is PROLOGUE:
            return total(what, self.steps[:k])
        return total(what, PROLOGUE) + (self.g - 1) * total(what, BODY) + total(what, self.steps[:k])

    def slot(self, what, k, ring):
        assert total(what, BODY) % ring == 0
        ahead = [] if self.steps is PROLOGUE else PROLOGUE
        return (total(what, ahead) + total(what, self.steps[:k])) % ring

    def by_tile(self, k):
        return self.steps is PROLOGUE and k == BY_TILE_STEP

    def factor(self, k, g):
        if self.steps is PROLOGUE:
            return list(FACTORS).index((k, g)), FACTORS[k, g]
        return self.before("relayed", k) + g, (self.slot("relayed", k, 2) + g) % 2

    def group(self, k):
        if self.steps is PROLOGUE:
            return 0
        return self.g - 1 if self.steps[k] == (2, 1) else self.g

    def relay_count(self, k):
        return 2 * self.group(k) + self.steps[k][0]


def cin_dlrm(nc, table, ids, first_row, w0a, w0b, w0c, w1, w2, wt1, bt1, wt2, bt2, wt3, dense, out):
    with ExitStack() as ctx:
        def sb(name, shape, dt=F32):
            return ctx.enter_context(nc.sbuf_tensor(name, shape, dt))

        def ps(name, shape):
            return ctx.enter_context(nc.psum_tensor(name, shape, F32))

        def sem(name):
            return ctx.enter_context(nc.semaphore(name))

        fields_dram = [nc.dram_tensor(f"fields{s}", (2 * FIELDS, PAIR), F32).ap() for s in range(STREAMS)]

        ids_sb = sb("ids_sb", [P, PAIRS * GATHERS], I32)
        first_sb = sb("first_sb", [P, GATHERS], I32)
        index = [sb(f"index{s}", [P, GATHERS], I32) for s in range(STREAMS)]
        gathered = [sb(f"gathered{s}", [P, GATHERS, DIM]) for s in range(STREAMS)]
        own = [sb(f"own{s}", [P, PAIR]) for s in range(STREAMS)]
        rotated = [sb(f"rotated{s}", [P, L0TILES, PAIR]) for s in range(STREAMS)]
        opposite = [sb(f"opposite{s}", [P, 2, QCOLS]) for s in range(STREAMS)]
        fields = [sb(f"fields_sb{s}", [P, TILES, PAIR]) for s in range(STREAMS)]
        hidden = [sb(f"hidden{s}", [P, HHALF, PAIR]) for s in range(STREAMS)]
        relu_out = [sb(f"relu_out{n}", [P, N]) for n in range(2)]
        vz = sb("vz", [P, ZRING, 2, PAIR])
        pz = sb("pz", [P, PRING, PAIR])
        w0a_sb = sb("w0a_sb", [P, L0TILES * HID])
        w0b_sb = sb("w0b_sb", [P, L0TILES * HID])
        w0c_sb = sb("w0c_sb", [P, MREP, HID])
        w_sb = [sb("w0_sb", [P, L0TILES, HID]),
                sb("w1_sb", [P, HHALF * TILES, HID]), sb("w2_sb", [P, HHALF * TILES, HID])]
        feats = [sb(f"feats{layer}", [P, PAIRS, CHUNK]) for layer in range(3)]
        stack01 = sb("stack01", [P, BATCH])
        stack2 = sb("stack2", [P, BATCH])
        wt1_sb = sb("wt1_sb", [P, F_TOP1])
        wt1d_sb = sb("wt1d_sb", [P, F_TOP1])
        wt2_sb = sb("wt2_sb", [P, F_TOP1 // P, F_TOP2])
        wt3_sb = sb("wt3_sb", [P, F_TOP2 // P])
        bt1_sb = sb("bt1_sb", [P, F_TOP1 // P])
        bt2_sb = sb("bt2_sb", [P, F_TOP2 // P])
        top1 = vz[:, 0, :, :].rearrange("p a (m n) -> p (a m) n", n=BATCH)
        top2 = vz[:, 1, 0, :].rearrange("p (m n) -> p m n", n=BATCH)
        y_sb = vz[0:1, 2, 0, 0:BATCH]

        factor = [ps(f"factor{n}", [P, PAIR]) for n in range(2)]
        acc = ps("acc", [P, 2, N])
        spare = ps("spare", [P, 2, N])

        factors = factor + [spare[:, :, :].rearrange("p a n -> p (a n)")]

        ids_in = sem("ids_in")
        index_ready = sem("index_ready")
        rows_in = [sem(f"rows_in{s}") for s in range(STREAMS)]
        scratch_in = [[sem(f"scratch_in{s}_{n}") for n in range(2)] for s in range(STREAMS)]
        own_in = [sem(f"own_in{s}") for s in range(STREAMS)]
        rotated_in = [[sem(f"rotated_in{s}_{t}") for t in range(L0TILES + 1)] for s in range(STREAMS)]
        fields_in = [[sem(f"fields_in{s}_{t}") for t in range(TILES)] for s in range(STREAMS)]
        w0_in, w0_ready, w1_in, w2_in = sem("w0_in"), sem("w0_ready"), sem("w1_in"), sem("w2_in")
        top_in, stack01_in, stack2_in = sem("top_in"), sem("stack01_in"), sem("stack2_in")
        factor_ready = sem("factor_ready")
        vz_ready, vz_used = sem("vz_ready"), sem("vz_used")
        pz_ready, pz_used = sem("pz_ready"), sem("pz_used")
        relu_done, sums_done = sem("relu_done"), sem("sums_done")
        relayed = [[sem(f"relayed{s}_{g}") for g in range(HHALF)] for s in range(STREAMS)]
        top1_ps, top1_done = sem("top1_ps"), sem("top1_done")
        top2_ps, top2_done = sem("top2_ps"), sem("top2_done")
        y_ps, y_done, out_done = sem("y_ps"), sem("y_done"), sem("out_done")

        def top1_bank(m):
            return factor[m // 2][:, (m % 2) * N:(m % 2 + 1) * N]

        block = ctx.enter_context(nc.Block())

        @block.sync
        def _(sp):
            sp.dma_start(ids_sb[:, :], ids).then_inc(ids_in, 16)
            sp.dma_start(first_sb[:, :], first_row).then_inc(ids_in, 16)
            sp.dma_start(w0a_sb[:, :], w0a).then_inc(w0_in, 16)
            sp.dma_start(w0b_sb[:, :], w0b).then_inc(w0_in, 16)
            sp.dma_start(w0c_sb[:, :, :], w0c).then_inc(w0_in, 16)
            sp.dma_start(w_sb[1][:, :, :], w1).then_inc(w1_in, 16)
            sp.dma_start(w_sb[2][:, :, :], w2).then_inc(w2_in, 16)

            sp.dma_start(wt1_sb[:, :], wt1[0:2 * HID, :]).then_inc(top_in, 16)
            sp.dma_start(wt1d_sb[0:HID + DIM, :], wt1[2 * HID:3 * HID + DIM, :]).then_inc(top_in, 16)
            sp.dma_start(stack2[HID:HID + DIM, :], dense).then_inc(top_in, 16)
            sp.dma_start(wt2_sb[:, :, :], wt2.rearrange("(m p) n -> p m n", p=P)).then_inc(top_in, 16)
            sp.dma_start(wt3_sb[:, :], wt3).then_inc(top_in, 16)
            sp.dma_start(bt1_sb[:, :], bt1).then_inc(top_in, 16)
            sp.dma_start(bt2_sb[:, :], bt2).then_inc(top_in, 16)

            def held(value, name):
                register = sp.alloc_register(f"sp_{name}")
                sp.reg_mov(register, value)
                return sp.snap(register)

            def named(values, name):
                return {k: v if isinstance(v, int) else held(v, f"{name}_{k}") for k, v in values.items()}

            def counts(s, g, last):
                values = {"rows": 16 * GATHERS * (g + 1), "loaded": 16 * (g + 1)}
                if last is not None:
                    values["read"] = 16 * g
                    values["rotated_used"] = last.before("vector", last.steps.index((0, s)) + 1)
                return named(values, f"rows{s}")

            def field_counts(s, g, name="fields"):
                values = {"loaded": 16 * (g + 1)}
                if not isinstance(g, int) or g:
                    layer2, k = (Section(BODY, g - 1), len(BODY)) if s == 0 else (Section(BODY, g), 2)
                    values["fields_used"] = layer2.before("vector", k)
                    values["fields_used_pool"] = layer2.before("pool", k)
                return named(values, f"{name}{s}")

            def to_scratch(s, value):
                sp.wait_ge(rows_in[s], value["rows"])
                if "read" in value:
                    for t in FIELDS_ORDER[-IN_FLIGHT:]:
                        sp.wait_ge(fields_in[s][t], value["read"])
                for n in range(2):
                    copy = fields_dram[s][n * FIELDS:(n + 1) * FIELDS, :]
                    sp.dma_start(copy.rearrange("m (q x) -> (m q) x", q=QUART),
                                 gathered[s][:, :, :].rearrange("p b d -> p (b d)")).then_inc(scratch_in[s][n], 16)

            def spread_rotated(s, value):
                sp.wait_ge(scratch_in[s][0], value["loaded"])
                if "rotated_used" in value:
                    sp.wait_ge(vz_ready, value["rotated_used"])
                span = fields_dram[s]
                sp.dma_start(own[s][:, :],
                             span[0:FIELDS, None, :].broadcast_to([FIELDS, MREP, PAIR])).then_inc(own_in[s], 16)
                sp.wait_ge(scratch_in[s][1], value["loaded"])
                sent = [own_in[s]]
                for t in range(L0TILES):
                    turn = bass.AP(span.tensor, span.offset + MREP * t * PAIR,
                                   [[PAIR, FIELDS], [PAIR, MREP], [1, PAIR]])
                    if len(sent) >= IN_FLIGHT:
                        sp.wait_ge(sent[-IN_FLIGHT], value["loaded"])
                    sp.dma_start(rotated[s][:, t, :], turn).then_inc(rotated_in[s][t], 16)
                    sent.append(rotated_in[s][t])
                both = bass.AP(span.tensor, span.offset, [[QCOLS, P], [FIELDS // 2 * PAIR, 2], [1, QCOLS]])
                sp.wait_ge(sent[-IN_FLIGHT], value["loaded"])
                sp.dma_start(opposite[s][:, :, :], both).then_inc(rotated_in[s][OPPOSITE], 16)

            def spread(s, value):
                to_scratch(s, value)
                spread_rotated(s, value)

            def spread_fields(s, value, first=0, end=TILES):
                span = fields_dram[s]
                if first == 0 and "fields_used" in value:
                    sp.wait_ge(vz_ready, value["fields_used"])
                    sp.wait_ge(pz_ready, value["fields_used_pool"])
                for n in range(first, end):
                    t = FIELDS_ORDER[n]
                    each = bass.AP(span.tensor, span.offset + MREP * t * PAIR,
                                   [[0, HROWS], [PAIR, MREP], [1, PAIR]])
                    if n >= IN_FLIGHT:
                        sp.wait_ge(fields_in[s][FIELDS_ORDER[n - IN_FLIGHT]], value["loaded"])
                    sp.dma_start(fields[s][:, t, :], each).then_inc(fields_in[s][t], 16)

            spread(0, counts(0, 0, None))
            pair0_fields, pair1_rows = field_counts(0, 0), counts(1, 0, None)
            spread_fields(0, pair0_fields, 0, FIRST_EARLY[0])
            to_scratch(1, pair1_rows)
            spread_fields(0, pair0_fields, *FIRST_EARLY)
            spread_rotated(1, pair1_rows)
            spread_fields(0, pair0_fields, FIRST_EARLY[1])
            spread_fields(1, field_counts(1, 0))
            spread(0, counts(0, 1, Section(PROLOGUE, 0)))
            spread_fields(0, field_counts(0, 1), 0, EARLY_FIELDS)
            spread(1, counts(1, 1, Section(PROLOGUE, 0)))
            with sp.Fori(1, GROUPS - 1) as g:
                now = [field_counts(s, g) for s in range(STREAMS)]
                after = [counts(s, g + 1, Section(BODY, g)) for s in range(STREAMS)]
                fields_after = field_counts(0, g + 1, "next_fields")
                spread_fields(0, now[0], EARLY_FIELDS)
                spread_fields(1, now[1])
                spread(0, after[0])
                spread_fields(0, fields_after, 0, EARLY_FIELDS)
                spread(1, after[1])
            spread_fields(0, field_counts(0, GROUPS - 1), EARLY_FIELDS)
            spread_fields(1, field_counts(1, GROUPS - 1))

            half_cols = BATCH // 2
            for layer in range(2):
                k = BODY.index((layer, 1))
                sp.wait_ge(sums_done, Section(BODY, GROUPS - 1).before("steps", k + 1))
                for ab in range(2):
                    sp.dma_start(stack01[layer * HID:(layer + 1) * HID, ab * half_cols:(ab + 1) * half_cols],
                                 feats[layer][ab * HID:(ab + 1) * HID, :, :].rearrange("p c j -> p (c j)")) \
                      .then_inc(stack01_in, 16)
            sp.wait_ge(sums_done, ALL_STEPS)
            for ab in range(2):
                sp.dma_start(stack2[0:HID, ab * half_cols:(ab + 1) * half_cols],
                             feats[2][ab * HID:(ab + 1) * HID, :, :].rearrange("p c j -> p (c j)")) \
                  .then_inc(stack2_in, 16)

        @block.gpsimd
        def _(pool):
            def start_gathers(s, g):
                pair = STREAMS * g + s
                nc.gpsimd.tensor_tensor(index[s][:, :], ids_sb[:, bass.ds(pair * GATHERS, GATHERS)],
                                        first_sb[:, :], ALU.add).then_inc(index_ready, 1)
                pool.wait_ge(index_ready, pair + 1)

            def gather(s, i):
                nc.gpsimd.indirect_dma_start(
                    gathered[s][:, i, :], None, table,
                    bass.IndirectOffsetOnAxis(ap=index[s][:, i:i + 1], axis=0)).then_inc(rows_in[s], 16)

            def products(section, k, plan):
                layer, s = section.steps[k]
                n0, slot0 = section.before("pool", k), section.slot("pool", k, PRING)
                units = pool_units(layer, section.by_tile(k))
                for gs, i0, _ in plan:
                    if i0 == 0:
                        g = 1 if section.steps is PROLOGUE else section.g + 1
                        for n in range(2):
                            pool.wait_ge(scratch_in[gs][n], 16 * g)
                        start_gathers(gs, g)
                todo = [(gs, i) for gs, i0, i1 in plan for i in range(i0, i1)]
                for u, (g, t) in enumerate(units):
                    if layer == 1 and g == 0:
                        pool.wait_ge(fields_in[s][t], 16 * (section.group(k) + 1))
                    if t == TILES - POOL_T:
                        pool.wait_ge(relayed[s][g], 32 * section.relay_count(k))
                    pool.wait_ge(pz_used, n0 + u + 1)
                    slot = (slot0 + u) % PRING
                    nc.gpsimd.tensor_tensor(pz[:, slot, :], fields[s][:, t, :], hidden[s][:, g, :],
                                            ALU.mult).then_inc(pz_ready, 1)
                    for gs, i in todo[len(todo) * u // len(units):len(todo) * (u + 1) // len(units)]:
                        gather(gs, i)
                if not units:
                    for gs, i in todo:
                        gather(gs, i)

            pool.wait_ge(ids_in, 32)
            for s in range(STREAMS):
                start_gathers(s, 0)
                for i in range(GATHERS):
                    gather(s, i)
            for k in range(len(PROLOGUE)):
                products(Section(PROLOGUE, 0), k, PROLOGUE_GATHERS.get(k, []))
            with pool.Fori(1, GROUPS - 1) as g:
                for k in range(len(BODY)):
                    products(Section(BODY, g), k, BODY_GATHERS.get(k, []))
            for k in range(len(BODY)):
                products(Section(BODY, GROUPS - 1), k, [])
            products(Section(END, GROUPS), 0, [])

        @block.vector
        def _(dve):
            dve.wait_ge(w0_in, 48)
            nc.vector.tensor_tensor(w_sb[0][:, :, :].rearrange("p t k -> p (t k)"), w0a_sb[:, :], w0b_sb[:, :],
                                    ALU.add).then_inc(w0_ready, 1)

            def products(section, k):
                layer, s = section.steps[k]
                n0, slot0 = section.before("vector", k), section.slot("vector", k, ZRING)
                at = -1
                for u, (g, t, nt) in enumerate(vector_units(layer, section.by_tile(k))):
                    put, fslot = section.factor(k, g)
                    if g != at:
                        dve.wait_ge(factor_ready, put + 1)
                        at = g
                    arrived = [rotated_in, fields_in, fields_in][layer][s]
                    for tile in range(t, t + nt):
                        if layer < 2 and g == 0:
                            dve.wait_ge(arrived[tile], 16 * (section.group(k) + 1))
                    if section.steps is not PROLOGUE or n0 + u >= ZRING:
                        dve.wait_ge(vz_used, n0 + u - ZRING + 1)
                    slot = (slot0 + u) % ZRING
                    if layer == 0 and t == OPPOSITE:
                        nc.vector.tensor_tensor(vz[:, slot, 0, 0:QCOLS], opposite[s][:, 0, :], opposite[s][:, 1, :],
                                                ALU.mult).then_inc(vz_ready, 1)
                        continue
                    src = rotated[s] if layer == 0 else fields[s]
                    nc.vector.tensor_tensor(vz[:, slot, 0:nt, :], src[:, t:t + nt, :],
                                            factors[fslot][:, None, :].broadcast_to([P, nt, PAIR]),
                                            ALU.mult).then_inc(vz_ready, 1)

            def dim_sums(layer, s, g, n, slot):
                dve.wait_ge(relu_done, n + 1)
                nc.vector.tensor_reduce(feats[layer][:, bass.ds(STREAMS * g + s, 1), :],
                                        relu_out[slot][:, :].rearrange("p (a b d) -> p a b d", a=1, d=DIM),
                                        op=ALU.add, axis=AX_X).then_inc(sums_done, 1)

            def sums_of(section, k):
                layer, s = section.steps[k]
                dim_sums(layer, s, section.group(k), section.before("steps", k), section.slot("steps", k, 2))

            def sums_before(section):
                n, slot = section.before("steps", 0) - 1, (section.slot("steps", 0, 2) + 1) % 2
                dim_sums(2, 0, section.g - 1, n, slot)

            for k in range(len(PROLOGUE)):
                products(Section(PROLOGUE, 0), k)
                if k:
                    sums_of(Section(PROLOGUE, 0), k - 1)
            with dve.Fori(1, GROUPS) as g:
                for k in range(len(BODY)):
                    products(Section(BODY, g), k)
                    if k:
                        sums_of(Section(BODY, g), k - 1)
                    else:
                        sums_before(Section(BODY, g))
            products(Section(END, GROUPS), 0)
            sums_before(Section(END, GROUPS))
            sums_of(Section(END, GROUPS), 0)

        @block.scalar
        def _(act):
            def put_factor(section, k):
                layer, s = section.steps[k]
                for g in range(SIZE["relayed"](layer)):
                    _, fslot = section.factor(k, g)
                    free = slot_free(section, k, g)
                    if not isinstance(free, int) or free:
                        act.wait_ge(vz_ready, free)
                    if layer == 0:
                        act.wait_ge(own_in[s], 16 * (section.group(k) + 1))
                        src = own[s][:, :]
                    else:
                        act.wait_ge(relayed[s][g], 32 * section.relay_count(k))
                        src = hidden[s][:, g, :]
                    nc.scalar.activation(factors[fslot][:, :], src, ACT.Copy).then_inc(factor_ready, 1)

            def slot_free(section, k, g):
                if section.steps is PROLOGUE:
                    put, slot = section.factor(k, g)
                    before = [held for held in list(FACTORS)[:put] if FACTORS[held] == slot]
                    if not before:
                        return 0
                    k0, g0 = before[-1]
                    units = vector_units(PROLOGUE[k0][0], section.by_tile(k0))
                    last = max(u for u, unit in enumerate(units) if unit[0] == g0)
                    return section.before("vector", k0) + last + 1
                start = section.before("vector", k)
                if g == 1:
                    return start
                layer = section.steps[k - 1][0] if k else 2
                halves = [h for h, _, _ in vector_units(layer)]
                return start - (halves.count(1) if 1 in halves else len(halves))

            def relu(section, k):
                n, slot = section.before("steps", k), section.slot("steps", k, 2)
                act.wait_ge(vz_used, section.before("vector", k + 1))
                if section.steps is not PROLOGUE or n >= 2:
                    act.wait_ge(sums_done, n - 1)
                nc.scalar.activation(relu_out[slot][:, :], acc[:, slot, :], ACT.Relu).then_inc(relu_done, 1)

            def relay(section, k):
                _, s = section.steps[k]
                n, slot = section.before("steps", k), section.slot("steps", k, 2)
                act.wait_ge(relu_done, n + 1)
                for g in range(HHALF):
                    for ab in range(2):
                        row = ab * HID + g * HROWS
                        act.dma_start(hidden[s][:, g, ab * N:(ab + 1) * N],
                                      relu_out[slot][row:row + HROWS, None, :]
                                      .broadcast_to([HROWS, MREP, N])).then_inc(relayed[s][g], 16)

            def relu_and_relay(section, k):
                relu(section, k)
                if section.steps[k][0] < 2:
                    relay(section, k)

            prologue = Section(PROLOGUE, 0)
            put_factor(prologue, 0)
            relu(prologue, 0)
            put_factor(prologue, 1)
            relay(prologue, 0)
            put_factor(prologue, 2)
            relu_and_relay(prologue, 1)
            for k in range(2, len(PROLOGUE)):
                if k + 1 < len(PROLOGUE):
                    put_factor(prologue, k + 1)
                else:
                    put_factor(Section(BODY, 1), 0)
                relu_and_relay(prologue, k)
            with act.Fori(1, GROUPS - 1) as g:
                for k in range(len(BODY)):
                    if k + 1 < len(BODY):
                        put_factor(Section(BODY, g), k + 1)
                    else:
                        put_factor(Section(BODY, g + 1), 0)
                    relu_and_relay(Section(BODY, g), k)
            for k in range(len(BODY)):
                if k + 1 < len(BODY):
                    put_factor(Section(BODY, GROUPS - 1), k + 1)
                else:
                    put_factor(Section(END, GROUPS), 0)
                relu_and_relay(Section(BODY, GROUPS - 1), k)
            relu(Section(END, GROUPS), 0)

            act.wait_ge(top_in, 112)
            for m in range(F_TOP1 // P):
                act.wait_ge(top1_ps, m + 1)
                nc.scalar.activation(top1[:, m, :], top1_bank(m),
                                     ACT.Relu, bias=bt1_sb[:, m:m + 1]).then_inc(top1_done, 1)
            for m in range(F_TOP2 // P):
                act.wait_ge(top2_ps, m + 1)
                nc.scalar.activation(top2[:, m, :], spare[:, m, :], ACT.Relu,
                                     bias=bt2_sb[:, m:m + 1]).then_inc(top2_done, 1)
            act.wait_ge(y_ps, 1)
            nc.scalar.activation(y_sb, acc[0:1, 0, :], ACT.Copy).then_inc(y_done, 1)
            act.wait_ge(y_done, 1)
            for ab in range(2):
                act.dma_start(out.rearrange("(c a j) o -> o a c j", a=2, j=CHUNK)[:, ab, :, :],
                              y_sb[:, ab * (BATCH // 2):(ab + 1) * (BATCH // 2)]
                              .rearrange("o (c j) -> o c j", j=CHUNK)).then_inc(out_done, 16)
            act.wait_ge(out_done, 32)

        @block.tensor
        def _(pe):
            pe.sem_inc(pz_used, PRING)

            def contract(section, k):
                layer, s = section.steps[k]
                n = section.before("steps", k)
                v0, vslot0 = section.before("vector", k), section.slot("vector", k, ZRING)
                p0, pslot0 = section.before("pool", k), section.slot("pool", k, PRING)
                bank = section.slot("steps", k, 2)
                if section.steps is not PROLOGUE or n >= 2:
                    pe.wait_ge(relu_done, n - 1)
                order = tensor_order(layer, section.by_tile(k))
                for at, (who, u) in enumerate(order):
                    if who == "v":
                        g, t, nt = vector_units(layer, section.by_tile(k))[u]
                        pe.wait_ge(vz_ready, v0 + u + 1)
                        slot = (vslot0 + u) % ZRING
                        pieces = [(g * TILES + t + j, vz[:, slot, j, :]) for j in range(nt)]
                    else:
                        g, t = pool_units(layer, section.by_tile(k))[u]
                        pe.wait_ge(pz_ready, p0 + u + 1)
                        pieces = [(g * TILES + t, pz[:, (pslot0 + u) % PRING, :])]
                    if layer == 0 and t == OPPOSITE:
                        for q in (0, 2, 1, 3):
                            ab, cols = q // 2, slice(q % 2 * QCOLS, (q % 2 + 1) * QCOLS)
                            last = nc.tensor.matmul(acc[ab * HID:(ab + 1) * HID, bank, cols], w0c_sb[:, q, :],
                                                    vz[:, slot, 0, 0:QCOLS], start=False, stop=q % 2 == 1)
                        pieces = []
                    for j, (kt, z) in enumerate(pieces):
                        start = at == 0 and j == 0
                        stop = at == len(order) - 1 and j == len(pieces) - 1
                        for ab in range(2):
                            last = nc.tensor.matmul(acc[ab * HID:(ab + 1) * HID, bank, :],
                                                    w_sb[layer][:, kt, :], z[:, ab * N:(ab + 1) * N],
                                                    start=start, stop=stop)
                    last.then_inc(vz_used if who == "v" else pz_used, 1)

            pe.wait_ge(w0_ready, 1)
            contract(Section(PROLOGUE, 0), 0)
            pe.wait_ge(w1_in, 16)
            pe.wait_ge(w2_in, 16)
            for k in range(1, len(PROLOGUE)):
                contract(Section(PROLOGUE, 0), k)
            with pe.Fori(1, GROUPS) as g:
                for k in range(len(BODY)):
                    contract(Section(BODY, g), k)
            contract(Section(END, GROUPS), 0)

            pe.wait_ge(top_in, 112)
            pe.wait_ge(stack01_in, 64)
            pe.wait_ge(vz_ready, Section(END, GROUPS).before("vector", 1))
            for m in range(F_TOP1 // P):
                nc.tensor.matmul(top1_bank(m), wt1_sb[:, m * P:(m + 1) * P], stack01[:, :], start=True, stop=False)
            pe.wait_ge(stack2_in, 32)
            for m in range(F_TOP1 // P):
                nc.tensor.matmul(top1_bank(m), wt1d_sb[0:HID + DIM, m * P:(m + 1) * P], stack2[0:HID + DIM, :],
                                 start=False, stop=True).then_inc(top1_ps, 1)
            for m in range(F_TOP2 // P):
                for j in range(F_TOP1 // P):
                    if m == 0:
                        pe.wait_ge(top1_done, j + 1)
                    last = nc.tensor.matmul(spare[:, m, :], wt2_sb[:, j, m * P:(m + 1) * P],
                                            top1[:, j, :], start=j == 0, stop=j == F_TOP1 // P - 1)
                last.then_inc(top2_ps, 1)
            for m in range(F_TOP2 // P):
                pe.wait_ge(top2_done, m + 1)
                last = nc.tensor.matmul(acc[0:1, 0, :], wt3_sb[:, m:m + 1], top2[:, m, :],
                                        start=m == 0, stop=m == F_TOP2 // P - 1)
            last.then_inc(y_ps, 1)


def kernel(**inputs):
    import numpy as np
    import concourse.bacc as bacc
    from concourse.bass_utils import run_bass_kernel_spmd

    tables = [inputs[f"tbl_{f}"] for f in range(FIELDS)]
    first = np.cumsum([0] + [t.shape[0] for t in tables[:-1]])
    table = np.concatenate([np.asarray(t) for t in tables], axis=0)
    ids = np.asarray(inputs["ids"]).reshape(PAIRS, QUART, GATHERS, FIELDS).transpose(3, 1, 0, 2)
    ids = np.ascontiguousarray(ids.reshape(P, PAIRS * GATHERS))
    first_row = np.repeat(np.repeat(first.astype(np.int32), QUART)[:, None], GATHERS, axis=1)
    w0 = np.asarray(inputs["L0_rec_W0"])
    w0a = np.zeros((FIELDS, MREP, L0TILES, HID), w0.dtype)
    w0b = np.zeros((FIELDS, MREP, L0TILES, HID), w0.dtype)
    h = np.arange(FIELDS)
    for r in range(FIELDS // 2):
        w0a[:, r % MREP, r // MREP] = w0[h, (h + r) % FIELDS]
        if r:
            w0b[:, r % MREP, r // MREP] = w0[(h + r) % FIELDS, h]

    w0c = np.zeros((FIELDS, MREP, MREP, HID), w0.dtype)
    for i in range(MREP):
        w0c[:, i, i] = w0[h, (h + FIELDS // 2) % FIELDS]

    def upper(w):
        w = np.asarray(w).reshape(TILES, MREP, HHALF, HROWS, HID).transpose(3, 1, 2, 0, 4)
        return np.ascontiguousarray(w.reshape(P, HHALF * TILES, HID))

    def columns(v, tiles):
        return np.ascontiguousarray(np.asarray(v).reshape(tiles, P).T)

    dense = np.asarray(inputs["dense_ctx"]).reshape(PAIRS, 2, CHUNK, DIM).transpose(3, 1, 0, 2)
    arrays = {
        "table": table, "ids": ids, "first_row": first_row,
        "w0a": w0a.reshape(P, -1), "w0b": w0b.reshape(P, -1),
        "w0c": w0c.reshape(P, MREP, HID),
        "w1": upper(inputs["L0_rec_W1"]), "w2": upper(inputs["L0_rec_W2"]),
        "wt1": np.asarray(inputs["W_top1"]), "bt1": columns(inputs["b_top1"], F_TOP1 // P),
        "wt2": np.asarray(inputs["W_top2"]), "bt2": columns(inputs["b_top2"], F_TOP2 // P),
        "wt3": columns(inputs["W_top3"], F_TOP2 // P),
        "dense": np.ascontiguousarray(dense.reshape(DIM, BATCH)),
    }
    nc = bacc.Bacc("TRN2", target_bir_lowering=False, num_devices=1)
    arrays = {f"in_{k}": np.ascontiguousarray(v) for k, v in arrays.items()}
    args = [nc.dram_tensor(k, v.shape, mybir.dt.from_np(v.dtype), kind="ExternalInput").ap()
            for k, v in arrays.items()]
    out = nc.dram_tensor("out_y", (BATCH, 1), F32, kind="ExternalOutput").ap()
    cin_dlrm(nc, *args, out)
    r = run_bass_kernel_spmd(nc, [arrays], core_ids=[0])
    return r.results[0]["out_y"]
```
